# Optimizing a Trainium2 kernel written in Bass

```python
import numpy as np
import jax
import jax.numpy as jnp

def _softmax(x, axis=-1):
    return jax.nn.softmax(x, axis=axis)

def _gelu(x):
    return jax.nn.gelu(x, approximate=True)

def _silu(x):
    return jax.nn.silu(x)

def _sigmoid(x):
    return jax.nn.sigmoid(x)

def _layernorm(x, axis=-1, eps=1e-05):
    m = jnp.mean(x, axis=axis, keepdims=True)
    v = jnp.var(x, axis=axis, keepdims=True)
    return (x - m) / jnp.sqrt(v + eps)

def _scatter_add(tgt, idx, src, axis=0):
    return tgt.at[idx].add(src)

def _segment_sum(src, seg, n):
    return jax.ops.segment_sum(src, seg, n)
kernel_name = 'mk_prb_d2_jaxref_r8_b279f3'

def setup_inputs(seed: int=0):
    np.random.seed(seed)
    _w = jnp.asarray

    def _L0_attn_setup():
        import jax, jax.numpy as jnp
        import numpy as np
        EMBED_DIM = 128
        NUM_HEADS = 16
        HEAD_DIM = EMBED_DIM // NUM_HEADS
        key = jax.random.key(seed)
        k0, k1, k2, k3, k4 = jax.random.split(key, 5)
        B, S = (1, 512)
        scale = 1.0 / np.sqrt(EMBED_DIM)
        x = jax.random.normal(k0, (B, S, EMBED_DIM), dtype=jnp.float32)
        Wqkv = jax.random.normal(k1, (EMBED_DIM, 3 * EMBED_DIM), dtype=jnp.float32) * scale
        bqkv = jax.random.normal(k2, (3 * EMBED_DIM,), dtype=jnp.float32) * 0.02
        Wout = jax.random.normal(k3, (EMBED_DIM, EMBED_DIM), dtype=jnp.float32) * scale
        bout = jax.random.normal(k4, (EMBED_DIM,), dtype=jnp.float32) * 0.02
        return {'x': x, 'Wqkv': Wqkv, 'bqkv': bqkv, 'Wout': Wout, 'bout': bout}
    _L0_attn_in = _L0_attn_setup()

    def _L0_ffn_setup():
        import jax, jax.numpy as jnp
        import numpy as np
        TOP_K = 2
        key = jax.random.key(seed)
        k1, k2, k3 = jax.random.split(key, 3)
        B, S, D, E = (8, 256, 128, 8)
        x = jax.random.normal(k1, (B, S, D), dtype=jnp.float32)
        gate_w = jax.random.normal(k2, (E, D), dtype=jnp.float32) * (1.0 / np.sqrt(D))
        gate_b = jnp.zeros((E,), dtype=jnp.float32)
        expert_w = jax.random.normal(k3, (E, D, D), dtype=jnp.float32) * (1.0 / np.sqrt(D))
        expert_b = jnp.zeros((E, D), dtype=jnp.float32)
        return {'x': x, 'gate_w': gate_w, 'gate_b': gate_b, 'expert_w': expert_w, 'expert_b': expert_b}
    _L0_ffn_in = _L0_ffn_setup()

    def _L1_attn_setup():
        import jax, jax.numpy as jnp
        import numpy as np
        B, S, H = (2, 256, 128)
        NUM_HEADS = 16
        HEAD_DIM = H // NUM_HEADS
        key = jax.random.key(seed)
        ks = jax.random.split(key, 5)
        sc = 1.0 / np.sqrt(H)
        return {'hidden_states': jax.random.normal(ks[0], (B, S, H), jnp.float32), 'Wq': jax.random.normal(ks[1], (H, H), jnp.float32) * sc, 'bq': jnp.zeros((H,), jnp.float32), 'Wk': jax.random.normal(ks[2], (H, H), jnp.float32) * sc, 'bk': jnp.zeros((H,), jnp.float32), 'Wv': jax.random.normal(ks[3], (H, H), jnp.float32) * sc, 'bv': jnp.zeros((H,), jnp.float32), 'Wg': jax.random.normal(ks[4], (H, 1), jnp.float32) * sc, 'bg': jnp.zeros((1,), jnp.float32)}
    _L1_attn_in = _L1_attn_setup()

    def _L1_ffn_setup():
        import jax, jax.numpy as jnp
        import numpy as np
        H, F, E_SHARED, E_ROUTED, K = (128, 512, 1, 8, 2)

        def _expert(x, w_up, w_down):
            h = jax.nn.gelu(jnp.einsum('bsh,hf->bsf', x, w_up), approximate=False)
            return jnp.einsum('bsf,fh->bsh', h, w_down)
        key = jax.random.key(seed)
        ks = jax.random.split(key, 6)
        x = jax.random.normal(ks[0], (4, 256, H), dtype=jnp.float32)
        s = 0.02
        shared_up = jax.random.normal(ks[1], (E_SHARED, H, F), dtype=jnp.float32) * s
        shared_down = jax.random.normal(ks[2], (E_SHARED, F, H), dtype=jnp.float32) * s
        routed_up = jax.random.normal(ks[3], (E_ROUTED, H, F), dtype=jnp.float32) * s
        routed_down = jax.random.normal(ks[4], (E_ROUTED, F, H), dtype=jnp.float32) * s
        router_w = jax.random.normal(ks[5], (H, E_ROUTED), dtype=jnp.float32) * s
        return {'x': x, 'shared_up': shared_up, 'shared_down': shared_down, 'routed_up': routed_up, 'routed_down': routed_down, 'router_w': router_w}
    _L1_ffn_in = _L1_ffn_setup()
    _d = {'L0_attn_x': _L0_attn_in['x'], 'L0_attn_Wqkv': _L0_attn_in['Wqkv'], 'L0_attn_bqkv': _L0_attn_in['bqkv'], 'L0_attn_Wout': _L0_attn_in['Wout'], 'L0_attn_bout': _L0_attn_in['bout'], 'L0_ffn_gate_w': _L0_ffn_in['gate_w'], 'L0_ffn_gate_b': _L0_ffn_in['gate_b'], 'L0_ffn_expert_w': _L0_ffn_in['expert_w'], 'L0_ffn_expert_b': _L0_ffn_in['expert_b'], 'L1_attn_Wq': _L1_attn_in['Wq'], 'L1_attn_bq': _L1_attn_in['bq'], 'L1_attn_Wk': _L1_attn_in['Wk'], 'L1_attn_bk': _L1_attn_in['bk'], 'L1_attn_Wv': _L1_attn_in['Wv'], 'L1_attn_bv': _L1_attn_in['bv'], 'L1_attn_Wg': _L1_attn_in['Wg'], 'L1_attn_bg': _L1_attn_in['bg'], 'L1_ffn_shared_up': _L1_ffn_in['shared_up'], 'L1_ffn_shared_down': _L1_ffn_in['shared_down'], 'L1_ffn_routed_up': _L1_ffn_in['routed_up'], 'L1_ffn_routed_down': _L1_ffn_in['routed_down'], 'L1_ffn_router_w': _L1_ffn_in['router_w']}
    _x0 = _d['L0_attn_x']
    _d['L0_attn_x'] = jax.random.normal(jax.random.fold_in(jax.random.key(seed), 1), (8, 512, 128), dtype=_x0.dtype)
    del _x0
    return _d

def reference(L0_attn_x, L0_attn_Wqkv, L0_attn_bqkv, L0_attn_Wout, L0_attn_bout, L0_ffn_gate_w, L0_ffn_gate_b, L0_ffn_expert_w, L0_ffn_expert_b, L1_attn_Wq, L1_attn_bq, L1_attn_Wk, L1_attn_bk, L1_attn_Wv, L1_attn_bv, L1_attn_Wg, L1_attn_bg, L1_ffn_shared_up, L1_ffn_shared_down, L1_ffn_routed_up, L1_ffn_routed_down, L1_ffn_router_w):

    def _L0_attn_ref(x, Wqkv, bqkv, Wout, bout):
        import jax, jax.numpy as jnp
        import numpy as np
        EMBED_DIM = 128
        NUM_HEADS = 16
        HEAD_DIM = EMBED_DIM // NUM_HEADS
        B, S, E = x.shape
        H, D = (NUM_HEADS, HEAD_DIM)
        qkv = x @ Wqkv + bqkv
        qkv = qkv.reshape(B, S, 3, H, D)
        q, k, v = (qkv[:, :, 0], qkv[:, :, 1], qkv[:, :, 2])
        softmax_scale = 1.0 / np.sqrt(D)
        scores = jnp.einsum('bthd,bshd->bhts', q, k * softmax_scale)
        causal_mask = jnp.triu(jnp.full((S, S), -10000.0, dtype=scores.dtype), 1)
        scores = scores + causal_mask
        attention = jax.nn.softmax(scores, axis=-1)
        context = jnp.einsum('bhts,bshd->bthd', attention, v)
        out = context.reshape(B, S, E) @ Wout + bout
        return out

    def _L0_ffn_ref(x, gate_w, gate_b, expert_w, expert_b):
        import jax, jax.numpy as jnp
        import numpy as np
        TOP_K = 2
        gate = jnp.einsum('bsd,ed->bse', x, gate_w) + gate_b
        _, idx = jax.lax.top_k(gate, TOP_K)
        E = gate_w.shape[0]
        flat_idx = idx.reshape(-1)
        counts = jnp.zeros((E,), dtype=x.dtype).at[flat_idx].add(1.0)
        expert_out = jax.nn.relu(jnp.einsum('bsd,ehd->bseh', x, expert_w) + expert_b)
        total = flat_idx.size
        out = jnp.einsum('bseh,e->bsh', expert_out, counts) / total
        return out

    def _L1_attn_ref(hidden_states, Wq, bq, Wk, bk, Wv, bv, Wg, bg):
        import jax, jax.numpy as jnp
        import numpy as np
        B, S, H = (2, 256, 128)
        NUM_HEADS = 16
        HEAD_DIM = H // NUM_HEADS
        b, s, h = hidden_states.shape
        g = jax.nn.sigmoid(hidden_states @ Wg + bg)
        Z_I = g
        Z_J = jnp.swapaxes(g, 1, 2)
        res = (1.0 - Z_I) * jnp.maximum(1.0 - Z_I - Z_J, 0.0) + Z_I * jnp.minimum(1.0 - Z_I + Z_J, 1.0)
        idx = jnp.arange(s)
        abs_ij = jnp.abs(idx[:, None] - idx[None, :]).astype(hidden_states.dtype)
        base = jnp.asarray(s - 2, hidden_states.dtype)
        scope = jnp.power(base, 1.0 - g) + 2.0 - abs_ij
        scope = jnp.clip(scope, 1e-32, 1.0)
        penalties = res * scope
        log_pen = jnp.log(jnp.maximum(penalties, 1e-32))

        def split_heads(x):
            return x.reshape(b, s, NUM_HEADS, HEAD_DIM).transpose(0, 2, 1, 3)
        q = split_heads(hidden_states @ Wq + bq)
        k = split_heads(hidden_states @ Wk + bk)
        v = split_heads(hidden_states @ Wv + bv)
        scores = jnp.einsum('bhqd,bhkd->bhqk', q, k) / np.sqrt(HEAD_DIM)
        scores = scores + log_pen[:, None, :, :]
        probs = jax.nn.softmax(scores, axis=-1)
        ctx = jnp.einsum('bhqk,bhkd->bhqd', probs, v)
        ctx = ctx.transpose(0, 2, 1, 3).reshape(b, s, h)
        return ctx

    def _L1_ffn_ref(x, shared_up, shared_down, routed_up, routed_down, router_w):
        import jax, jax.numpy as jnp
        import numpy as np
        H, F, E_SHARED, E_ROUTED, K = (128, 512, 1, 8, 2)

        def _expert(x, w_up, w_down):
            h = jax.nn.gelu(jnp.einsum('bsh,hf->bsf', x, w_up), approximate=False)
            return jnp.einsum('bsf,fh->bsh', h, w_down)
        shared_out = jnp.zeros_like(x)
        for i in range(E_SHARED):
            shared_out = shared_out + _expert(x, shared_up[i], shared_down[i])
        probs = jax.nn.softmax(jnp.einsum('bsh,he->bse', x, router_w), axis=-1)
        top_k_prob, top_k_idx = jax.lax.top_k(probs, K)
        onehot = jax.nn.one_hot(top_k_idx, E_ROUTED, dtype=x.dtype)
        gates = jnp.einsum('bsk,bske->bse', top_k_prob, onehot)
        routed_out = jnp.zeros_like(x)
        for e in range(E_ROUTED):
            y = _expert(x, routed_up[e], routed_down[e])
            routed_out = routed_out + gates[..., e:e + 1] * y
        return shared_out + routed_out + x
    x = L0_attn_x
    xn = _layernorm(x, axis=-1)
    x = x + _L0_attn_ref(xn, L0_attn_Wqkv, L0_attn_bqkv, L0_attn_Wout, L0_attn_bout) + _L0_ffn_ref(xn, L0_ffn_gate_w, L0_ffn_gate_b, L0_ffn_expert_w, L0_ffn_expert_b)
    xn = _layernorm(x, axis=-1)
    x = x + _L1_attn_ref(xn, L1_attn_Wq, L1_attn_bq, L1_attn_Wk, L1_attn_bk, L1_attn_Wv, L1_attn_bv, L1_attn_Wg, L1_attn_bg) + _L1_ffn_ref(xn, L1_ffn_shared_up, L1_ffn_shared_down, L1_ffn_routed_up, L1_ffn_routed_down, L1_ffn_router_w)
    return x

_drawn_inputs = setup_inputs


def setup_inputs(seed=0):
    import zlib

    import numpy as np

    out = dict(_drawn_inputs(seed))
    spreads = {'L0_ffn_gate_b': (0.0, 0.282),
     'L0_ffn_expert_b': (0.0, 0.295),
     'L1_attn_bq': (0.0, 0.664),
     'L1_attn_bk': (0.0, 2.0),
     'L1_attn_bv': (0.0, 0.276)}
    factors = {'L1_ffn_routed_up': 8.0,
     'L1_ffn_routed_down': 8.0,
     'L1_ffn_router_w': 8.0,
     'L1_ffn_shared_up': 3.778,
     'L1_ffn_shared_down': 3.708}
    for name, (base, spread) in spreads.items():
        noise = np.random.default_rng([zlib.crc32(name.encode()), seed]).standard_normal(out[name].shape)
        drawn = base * np.exp(spread * noise) if base else spread * noise
        out[name] = jnp.asarray(drawn.astype(out[name].dtype))
    for name, factor in factors.items():
        out[name] = (out[name] * factor).astype(out[name].dtype)
    return out
```

```python
from contextlib import ExitStack

import numpy as np

import concourse.bass as bass
from concourse import mybir

ALU = mybir.AluOpType
ACT = mybir.ActivationFunctionType
AX = mybir.AxisListType
F32 = mybir.dt.float32
BF16 = mybir.dt.bfloat16
F16 = mybir.dt.float16

P = 128
B, S, D = 8, 512, 128
NH, HD = 16, 8
NT = B * S // P
KB = S // P
NG, HG = 4, 4
UN = KB * HG
E = 8
F = 512
FC = F // P
EPS = 1e-5
KROWS = 72
SHIFT_ROW = 96
PRING = 8
LAG = (3, 6)
TOKENS = B * S
LOADS = 15 + 4 * HD
ON_DVE = (2, 6, 10, 14)

N_POOL = UN - len(ON_DVE)

SPARE = (
    {"every": {2: "maxima", 7: "contexts"},
     "next": {(0, 10): "q", (0, 12): "k", (0, 14): "v"}},
    {"every": {2: "maxima", 10: "contexts"},
     "next": {(0, 7): "q", (0, 13): "k", (0, 15): "v", (1, 7): "gate", (1, 13): "gates",
              (2, 7): "penalty0", (2, 13): "penalty1", (3, 7): "penalty2", (3, 13): "penalty3"}},
)
SCALAR_NEXT = (
    {(0, 5): "xb", (0, 11): "q", (0, 12): "q_hi", (0, 13): "k", (0, 14): "k_hi", (0, 15): "q_mid", (1, 0): "k_mid"},
    {(0, 5): "xb", (0, 8): "q", (0, 9): "q_hi", (0, 13): "q_mid", (0, 14): "k", (0, 15): "k_hi", (1, 2): "k_mid",
     (1, 8): "gate", (1, 12): "reach", (1, 14): "gates",
     (1, 15): "u0", (2, 0): "t0", (2, 1): "s0", (2, 8): "raw0", (2, 5): "u1", (2, 6): "t1", (2, 7): "s1", (2, 14): "raw1",
     (2, 12): "u2", (2, 13): "t2", (2, 15): "s2", (3, 8): "raw2", (3, 2): "u3", (3, 3): "t3", (3, 5): "s3",
     (3, 14): "raw3"},
)
VECTOR_NEXT = (
    {(0, 13): "q_res", (0, 15): "k_res", (1, 0): "v", (1, 1): "q_lo", (1, 2): "k_lo"},
    {(0, 12): "q_res", (0, 14): "q_lo", (1, 0): "v", (1, 1): "k_res", (1, 4): "k_lo", (1, 10): "gate",
     (2, 2): "sum0", (2, 3): "product0", (2, 9): "sum1", (2, 10): "product1",
     (3, 0): "sum2", (3, 1): "product2", (3, 8): "sum3", (3, 9): "product3", (3, 15): "put0"},
)


class Chain:

    def __init__(self, eng, sem):
        self.eng, self.sem, self.base, self.k = eng, sem, 0, 0

    def link(self, ins):
        self.k += 1
        ins.then_inc(self.sem, 1)
        self.eng.wait_ge(self.sem, self.base + self.k)

    def start(self, base):
        self.base, self.k = base, 0

    def fill(self, per):
        assert self.k <= per, self.k
        if self.k < per:
            self.eng.sem_inc(self.sem, per - self.k)


def program(nc, io, out):
    ctx = ExitStack()
    with ctx:
        def sb(name, shape, dt=F32):
            return ctx.enter_context(nc.sbuf_tensor(name, shape, dt))

        def sem(name):
            return ctx.enter_context(nc.semaphore(name))

        x = sb("x", [P, NT, D])
        xnT = sb("xnT", [P, TOKENS])
        big = sb("big", [P, 16 * S])
        context = big[:, 0:NT * D].rearrange("p (t d) -> p t d", t=NT)
        penalty = big[:, 0:KB * S].rearrange("p (k q) -> p k q", k=KB)
        penalty_raw = big[:, KB * S:2 * KB * S].rearrange("p (k q) -> p k q", k=KB)
        qst = sb("qst", [P, NG, HG * S], BF16)
        kst = sb("kst", [P, NG, HG * S], BF16)
        probs = sb("probs", [P, PRING, S])
        parts = sb("parts", [P, 6, S], BF16)
        qk_f = sb("qk_f", [P, 2, S])
        qk_r = sb("qk_r", [P, 2, S])
        vexp = sb("vexp", [P, NG, KB, HG, 32])
        vtok = sb("vtok", [P, KB, NH, HD])
        xb = sb("xb", [P, S])
        av_s = sb("av_s", [P, S])
        mx = sb("mx", [P, NG, UN])
        mrow = sb("mrow", [UN, NG, 2, P], BF16)
        wproj = sb("wproj", [P, 2, 3, D])
        wraw = big[:, 6144:6144 + 2 * 3 * D].rearrange("p (l t n) -> p l t n", l=2, t=3)
        wout = sb("wout", [P, D])
        bqk = sb("bqk", [P, 2, 2])
        bv = sb("bv", [P, 2, D])
        bo = sb("bo", [P, 1])
        ident = sb("ident", [P, P])
        ident16 = sb("ident16", [P, P], F16)
        mask_q = sb("mask_q", [P, P], F16)
        mask_k = sb("mask_k", [P, P], F16)
        ones = sb("ones", [P, P])
        dist = sb("dist", [P, 2 * S - P])
        disti = big[:, 7168:7168 + 2 * S - P].bitcast(mybir.dt.int32)
        stats = sb("stats", [P, NT, 6])
        lnw = sb("lnw", [P, 5, NT])
        xn = qk_r[:, 0, :].rearrange("p (t d) -> p t d", t=4)
        xts = qk_r[:, 1, :].rearrange("p (t d) -> p t d", t=4)
        wgate = sb("wgate", [P, 2, E])
        bgate = sb("bgate", [P, E])
        eidx = sb("eidx", [P, E])
        eidx_i = sb("eidx_i", [P, E], mybir.dt.int32)
        gt = sb("gt", [P, 4, NT, E])
        gs = sb("gs", [P, 4, NT])
        cnt = sb("cnt", [P, E])
        ew = big[:, 4096:5120].rearrange("p (e d) -> p e d", e=E)
        ewT = big[:, 5120:6144].rearrange("p (e d) -> p e d", e=E)
        eb = sb("eb", [P, E])
        nb = sb("nb", [P, E])
        bsum = sb("bsum", [P, 1])
        rec = sb("rec", [P, KB, HG])
        ctx_t = sb("ctx_t", [P, KB, HG, HD])
        wg = sb("wg", [P, 1])
        bg = sb("bg", [P, 1])
        nbg = sb("nbg", [P, 1])
        zc = sb("zc", [P, 7, KB])
        lnbase = sb("lnbase", [P, 1])
        zrow = sb("zrow", [P, S])
        pw = sb("pw", [P, 4, S])

        banks = [ctx.enter_context(nc.psum_tensor(f"bank{i}", [P, S], F32)) for i in range(8)]
        mxb, scb, avb, m0 = banks[0:3], banks[3:5], banks[5:7], banks[7]
        scratch = nc.dram_tensor("qk_parts", [6, P, S], BF16, kind="Internal")

        d_x, d_w, d_out = sem("d_x"), sem("d_w"), sem("d_out")
        consts = sem("consts")
        wready = sem("wready")
        ch = {n: sem(f"chain_{n}") for n in ("vector", "scalar", "gpsimd")}
        var_ok = [sem(f"var_ok{l}") for l in (0, 1)]
        std_ok = [sem(f"std_ok{l}") for l in (0, 1)]
        xn_ok = [sem(f"xn_ok{l}") for l in (0, 1)]
        tr_ok = [sem(f"tr_ok{l}") for l in (0, 1)]
        xts_ok = [sem(f"xts_ok{l}") for l in (0, 1)]
        xnT_ok = [sem(f"xnT_ok{l}") for l in (0, 1)]
        logits_ok = [sem(f"logits_ok{l}") for l in (0, 1)]
        xadd_ok = sem("xadd_ok")
        g_sub, g_exp, mask_ok, cnt_ps, cnt_ok, ewT_ps, ewT_ok = (
            sem(n) for n in ("g_sub", "g_exp", "mask_ok", "cnt_ps", "cnt_ok", "ewT_ps", "ewT_ok"))
        A = []
        for l in (0, 1):
            names = ("stacked0 stacked1 stacked2 stacked3 shift0 shift1 shift2 shift3 spilled xb_ok "
                     "qk_ps q_used k_used hi_ok res_ok mid_ok lo_ok v_ps v_ok vexp_ok "
                     "mx_ps mx_ok mt_ps mhi_ok mrow_ok reach_ok sc_ps exp_ok pen_v pen_p av_ps "
                     "av_s_ok avt_ps norm_ok zc_ps ze_ok zc_ok zr_ps zr_ok penx_ok penq_ok "
                     "pent_ps penraw_ok pen_ok").split()
            A.append({n: sem(f"{n}_{l}") for n in names})
        ctile_ok, ct_ps, ctT_ok, op_ps, acc0_ok, ff_ps, acc_ok, yT_ps, x1_ok = (
            sem(n) for n in ("ctile_ok", "ct_ps", "ctT_ok", "op_ps", "acc0_ok", "ff_ps", "acc_ok", "yT_ps", "x1_ok"))
        w_in = [sem("w_in0"), sem("w_in1")]
        up_ps, hid_ok, dn_ps, add_ok = (sem(n) for n in ("up_ps", "hid_ok", "dn_ps", "add_ok"))

        block = ctx.enter_context(nc.Block())

        def n_slot(u):
            return u % PRING

        def max_bank(g, u):
            return mxb[(UN * g + u) % 3]

        def max_bank_last(g, u):
            i = UN * g + u
            return 3 if i >= 3 else (1, 4, 4)[i]

        def over_batches(eng, body):
            body(0, True, False)
            with eng.Fori(1, B - 1) as b:
                body(b, False, False)
            body(B - 1, False, True)

        def unit_key(u):
            return u // HG, u % HG

        def unit_query(u):
            return u // KB, u % KB

        w_up = [big[:, i * 1024:i * 1024 + 512] for i in range(2)]
        w_dn = [big[:, i * 1024 + 512:i * 1024 + 1024].rearrange("p (c h) -> p c h", c=FC) for i in range(2)]
        hidden = [big[:, 2048 + i * 2048:4096 + i * 2048].rearrange("p (c q) -> p c q", c=FC) for i in range(2)]

        @block.sync
        def _(sp):
            for c in range(4):
                sp.dma_start(x[:, c * 8:(c + 1) * 8, :],
                             io["x"].rearrange("b s d -> (b s) d").rearrange("(t p) d -> p t d", p=P)[:, c * 8:(c + 1) * 8, :]
                             ).then_inc(d_x, 16)
            for l in (0, 1):
                a = A[l]

                def spill(b):
                    if not (isinstance(b, int) and b == 0):
                        for g in range(NG):
                            sp.wait_ge(a[f"stacked{g}"], 96 * b)
                    sp.wait_ge(a["lo_ok"], 2 * b + 2)
                    sp.dma_start(scratch.ap().rearrange("s p q -> p s q"), parts[:, :, :]).then_inc(a["spilled"], 16)
                    sp.wait_ge(a["spilled"], 16 * b + 16)

                def stack(g):
                    for so in range(3):
                        rows = slice(24 * so, 24 * so + 24)
                        q_src = bass.AP(tensor=scratch.ap().tensor, offset=so * P * S + g * HG * S,
                                        ap=[[0, 3], [NH * S, HD], [1, HG * S]])
                        k_src = bass.AP(tensor=scratch.ap().tensor, offset=3 * P * S + g * HG * S,
                                        ap=[[P * S, 3], [NH * S, HD], [1, HG * S]])
                        sp.dma_start(qst[rows, g, :], q_src).then_inc(a[f"stacked{g}"], 16)
                        sp.dma_start(kst[rows, g, :], k_src).then_inc(a[f"stacked{g}"], 16)

                def shift(G, g):
                    sp.wait_ge(a["mrow_ok"], G + 1)
                    for r in range(2):
                        sp.dma_start(qst[SHIFT_ROW + r:SHIFT_ROW + r + 1, g, :], mrow[0:UN, g, r, :]
                                     ).then_inc(a[f"shift{g}"], 16)

                spill(0)
                for g in range(NG):
                    stack(g)
                shift(0, 0)

                def body(b, first, last):
                    for g in range(NG):
                        G = 4 * b + g
                        if not (first if g == 0 else last):
                            if g == 1:
                                spill(b + 1)
                            sp.wait_ge(a["sc_ps"], UN * G)
                            stack((g - 1) % NG)
                        if not (last and g == NG - 1):
                            shift(G + 1, (g + 1) % NG)

                over_batches(sp, body)
            sp.wait_ge(A[1]["norm_ok"], B * NG)
            for e in range(E + 1):
                if e >= 2:
                    sp.wait_ge(dn_ps, B * (e - 1))
                up = io["shared_up"][0] if e == 0 else io["routed_up"][e - 1]
                dn = io["shared_down"][0] if e == 0 else io["routed_down"][e - 1]
                sp.dma_start(w_up[e % 2], up).then_inc(w_in[e % 2], 16)
                sp.dma_start(w_dn[e % 2], dn.rearrange("(c p) h -> p c h", p=P)).then_inc(w_in[e % 2], 16)
            for b in range(B):
                sp.wait_ge(add_ok, 2 + B * E + b + 1)
                sp.dma_start(out[b].rearrange("(t p) d -> p t d", p=P), x[:, 4 * b:4 * b + 4, :]).then_inc(d_out, 16)
            sp.wait_ge(d_out, 16 * B)

        @block.gpsimd
        def _(pool):
            chain = Chain(pool, ch["gpsimd"])
            link = chain.link
            link(nc.gpsimd.memset(ident[:, :], 0.0))
            nc.gpsimd.affine_select(out=ident[:, :], in_=ident[:, :], compare_op=ALU.not_equal, fill=1.0,
                                    base=0, pattern=[[-1, P]], channel_multiplier=1).then_inc(consts, 1)
            link(nc.gpsimd.memset(ident16[:, :], 0.0))
            nc.gpsimd.affine_select(out=ident16[:, :], in_=ident16[:, :], compare_op=ALU.not_equal, fill=1.0,
                                    base=0, pattern=[[-1, P]], channel_multiplier=1).then_inc(consts, 1)
            link(nc.gpsimd.memset(mask_q[:, :], 0.0))
            nc.gpsimd.affine_select(out=mask_q[:, :], in_=mask_q[:, :], compare_op=ALU.is_ge, fill=-10000.0,
                                    base=0, pattern=[[-1, P]], channel_multiplier=1).then_inc(consts, 1)
            link(nc.gpsimd.memset(mask_k[:, :], 0.0))
            nc.gpsimd.affine_select(out=mask_k[:, :], in_=mask_k[:, :], compare_op=ALU.is_ge, fill=-10000.0,
                                    base=0, pattern=[[1, P]], channel_multiplier=-1).then_inc(consts, 1)
            nc.gpsimd.memset(ones[:, :], 1.0).then_inc(consts, 1)
            nc.gpsimd.memset(lnbase[:, :], float(np.log(S - 2.0))).then_inc(consts, 1)
            nc.gpsimd.iota(eidx_i[:, :], pattern=[[1, E]], base=-E, channel_multiplier=0).then_inc(consts, 1)
            nc.gpsimd.iota(disti[:, :], pattern=[[1, 2 * S - P]], base=-(S - P), channel_multiplier=-1).then_inc(consts, 1)
            pool.wait_ge(consts, 8)
            nc.gpsimd.memset(qst[64:SHIFT_ROW, :, :], 0.0).then_inc(consts, 1)
            pool.wait_ge(consts, 9)
            nc.gpsimd.memset(kst[64:SHIFT_ROW, :, :], 0.0).then_inc(consts, 1)
            pool.wait_ge(consts, 10)
            nc.gpsimd.memset(kst[SHIFT_ROW:SHIFT_ROW + 2, :, :], 1.0).then_inc(consts, 1)
            pool.wait_ge(consts, 11)
            link(nc.gpsimd.memset(vexp[:, :, :, :, HD + 1:32], 0.0))
            nc.gpsimd.memset(vexp[:, :, :, :, HD:HD + 1], 1.0).then_inc(consts, 1)

            a = A[1]
            in_pool = [u for u in range(UN) if u not in ON_DVE]
            def body(b, first, last):
                for g in range(NG):
                    G = 4 * b + g
                    for u in range(UN):
                        if u in in_pool:
                            kb = unit_key(u)[0]
                            n = UN * G + u
                            if g == 0:
                                pool.wait_ge(a["pen_ok"], KB * b + kb + 1)
                            pool.wait_ge(a["exp_ok"], n + 1)
                            t = probs[:, n_slot(u), :]
                            nc.gpsimd.tensor_tensor(t, t, penalty[:, kb, :], ALU.mult).then_inc(a["pen_p"], 1)

            over_batches(pool, body)

        @block.scalar
        def _(act):
            chain = Chain(act, ch["scalar"])
            link = chain.link
            with nc.allow_non_contiguous_dma(reason="small bias and gate loads"):
                loads = [
                    (wraw[:, 0, :, :], io["Wqkv"].rearrange("k (t n) -> k t n", t=3)),
                    (wraw[:, 1, 0, :], io["Wq"]), (wraw[:, 1, 1, :], io["Wk"]), (wraw[:, 1, 2, :], io["Wv"]),
                    (wout[:, :], io["Wout"]),
                    (ew[:, :, :], io["expert_w"].rearrange("e h d -> h e d")),
                    (wgate[:, 0, :], io["gate_w"].rearrange("e d -> d e")),
                    (wgate[:, 1, :], io["router_w"]),
                    (bgate[:, :], io["gate_b"].partition_broadcast(P)),
                    (eb[:, :], io["expert_b"].rearrange("e h -> h e")),
                    (bv[:, 0, :], io["bqkv"][2 * D:3 * D].partition_broadcast(P)),
                    (bv[:, 1, :], io["bv"].partition_broadcast(P)),
                    (bo[:, :], io["bout"].rearrange("(n o) -> n o", o=1)),
                    (wg[:, :], io["Wg"]),
                    (bg[:, :], io["bg"].partition_broadcast(P)),
                ]
                for l, t, v in ((0, 0, io["bqkv"][0:D]), (0, 1, io["bqkv"][D:2 * D]), (1, 0, io["bq"]), (1, 1, io["bk"])):
                    for d in range(HD):
                        loads.append((bqk[d * NH:(d + 1) * NH, l, t:t + 1],
                                      v.rearrange("(h d) -> d h", d=HD)[d].rearrange("(h o) -> h o", o=1)))
                for dst, src in loads:
                    act.dma_start(dst, src).then_inc(d_w, 16)
                assert len(loads) == LOADS

            def norm_scalar(l):
                act.wait_ge(var_ok[l], 1)
                nc.scalar.activation(lnw[:, 4, :], lnw[:, 3, :], ACT.Sqrt).then_inc(std_ok[l], 1)

                def body(b, first):
                    for i in range(2):
                        act.wait_ge(tr_ok[l], 2 * b + i + 1)
                        if not first:
                            act.wait_ge(xnT_ok[l], 2 * b + i - 1)
                        nc.scalar.activation(xts[:, 2 * i:2 * i + 2, :],
                                             banks[i][:, 0:2 * P].rearrange("p (a c) -> p a c", a=2),
                                             ACT.Copy).then_inc(xts_ok[l], 1)

                body(0, True)
                with act.Fori(1, B) as b:
                    body(b, False)

            def attention_scalar(l):
                a = A[l]

                def prepare(b, what):
                    if what == "xb":
                        nc.scalar.activation(xb[:, :], xnT[:, bass.ds(b * S, S)], ACT.Copy).then_inc(a["xb_ok"], 1)
                        return
                    t = 0 if what[0] == "q" else 1
                    if what in ("q", "k"):
                        act.wait_ge(a["qk_ps"], 2 * b + t + 1)
                        nc.scalar.activation(qk_f[:, t, :], m0[:, :], ACT.Identity, bias=bqk[:, l, t:t + 1],
                                             scale=(1.0, HD ** -0.5)[t]).then_inc(a[what + "_used"], 1)
                    elif what in ("q_hi", "k_hi"):
                        act.wait_ge(a[what[0] + "_used"], b + 1)
                        nc.scalar.activation(parts[:, 3 * t, :], qk_f[:, t, :], ACT.Copy).then_inc(a["hi_ok"], 1)
                    elif what in ("q_mid", "k_mid"):
                        act.wait_ge(a["res_ok"], 2 * b + t + 1)
                        nc.scalar.activation(parts[:, 3 * t + 1, :], qk_r[:, t, :], ACT.Copy).then_inc(a["mid_ok"], 1)
                    elif what == "gate":
                        act.wait_ge(a["zc_ps"], b + 1)
                        nc.scalar.activation(zc[:, 0, :], m0[:, 0:KB], ACT.Exp, bias=nbg[:, :], scale=-1.0
                                             ).then_inc(a["ze_ok"], 1)
                    elif what == "reach":
                        act.wait_ge(a["zc_ok"], b + 1)
                        nc.scalar.activation(zc[:, 6, :], zc[:, 1, :], ACT.Exp, scale=-float(np.log(S - 2.0)),
                                             bias=lnbase[:, :]).then_inc(a["reach_ok"], 1)
                    elif what == "gates":
                        act.wait_ge(a["zr_ps"], b + 1)
                        nc.scalar.activation(zrow[:, :], m0[:, :], ACT.Copy).then_inc(a["zr_ok"], 1)
                    else:
                        i = int(what[-1])
                        n = KB * b + i
                        if what[:-1] == "u":
                            if i == 0:
                                act.wait_ge(a["zr_ok"], b + 1)
                            if not (isinstance(b, int) and n == 0):
                                act.wait_ge(a["penq_ok"], n)
                            nc.scalar.activation(pw[:, 0, :], zrow[:, :], ACT.Relu, scale=zc[:, 2, i:i + 1],
                                                 bias=zc[:, 3, i:i + 1])
                        elif what[:-1] == "t":
                            nc.scalar.activation(pw[:, 1, :], zrow[:, :], ACT.Relu, scale=zc[:, 5, i:i + 1],
                                                 bias=zc[:, 4, i:i + 1])
                        elif what[:-1] == "s":
                            if i == 0:
                                act.wait_ge(a["reach_ok"], b + 1)
                            lo = (KB - 1 - i) * P
                            nc.scalar.activation(pw[:, 2, :], dist[:, lo:lo + S], ACT.Identity,
                                                 bias=zc[:, 6, i:i + 1]).then_inc(a["penx_ok"], 1)
                        elif what[:-1] == "raw":
                            act.wait_ge(a["pent_ps"], n + 1)
                            if i == 0 and not (isinstance(b, int) and b == 0):
                                act.wait_ge(a["pen_ok"], KB * b)
                            nc.scalar.activation(penalty_raw[:, :, i * P:(i + 1) * P],
                                                 m0[:, :].rearrange("p (k q) -> p k q", k=KB), ACT.Copy
                                                 ).then_inc(a["penraw_ok"], 1)

                def put_v(g):
                    nc.scalar.activation(vexp[:, g, :, :, 0:HD], vtok[:, :, HG * g:HG * g + HG, :], ACT.Copy
                                         ).then_inc(a["vexp_ok"], 1)

                def shift_hi(G, g):
                    act.wait_ge(a["mt_ps"], G + 1)
                    nc.scalar.activation(mrow[:, g, 0, :], m0[0:UN, 0:P], ACT.Copy, scale=-1.0).then_inc(a["mhi_ok"], 1)

                for what in ("xb", "q", "q_hi", "k", "k_hi", "q_mid", "k_mid"):
                    prepare(0, what)
                act.wait_ge(a["v_ok"], 1)
                for g in range(NG):
                    put_v(g)
                if l == 1:
                    for what in ("gate", "reach", "gates"):
                        prepare(0, what)
                    for i in range(KB):
                        for what in "uts":
                            prepare(0, f"{what}{i}")
                        prepare(0, f"raw{i}")
                shift_hi(0, 0)
                lag = LAG[l]

                def tail(G, g):
                    act.wait_ge(a["av_ps"], UN * G)
                    if not isinstance(G, int) or G >= 2:
                        act.wait_ge(a["avt_ps"], G - 1)
                    nc.scalar.activation(av_s[:, :], avb[g % 2][:, :], ACT.Copy).then_inc(a["av_s_ok"], 1)

                def body(b, first, last):
                    for g in range(NG):
                        G = 4 * b + g
                        for u in range(UN):
                            n = UN * G + u
                            act.wait_ge(a["sc_ps"], n + 1)
                            if not first or UN * g + u >= PRING:
                                act.wait_ge(a["av_ps"], n - PRING + 1)
                            lo = unit_key(u)[0] * P if l == 0 else 0
                            nc.scalar.activation(probs[:, n_slot(u), lo:S], scb[u % 2][:, 0:S - lo], ACT.Exp
                                                 ).then_inc(a["exp_ok"], 1)
                            if u == 4 and not (last and g == NG - 1):
                                shift_hi(G + 1, (g + 1) % NG)
                            if u == lag + 1 and not (first and g == 0):
                                tail(G, (g - 1) % NG)
                            if u == lag + 2 and not (first if g == 0 else last):
                                act.wait_ge(a["v_ok"], (b if g == 0 else b + 1) + 1)
                                put_v((g - 1) % NG)
                            if last:
                                continue
                            what = SCALAR_NEXT[l].get((g, u))
                            if what == "xb":
                                act.wait_ge(a["v_ps"], b + 1)
                                if l == 1:
                                    act.wait_ge(a["zc_ps"], b + 1)
                            if what == "q_hi":
                                act.wait_ge(a["spilled"], 16 * (b + 1))
                            if what:
                                prepare(b + 1, what)

                over_batches(act, body)
                tail(B * NG, (NG - 1) % NG)

            norm_scalar(0)
            for e in range(E):
                act.wait_ge(ewT_ps, e // 4 + 1)
                if e == 0:
                    act.wait_ge(cnt_ok, 1)
                nc.scalar.activation(ewT[:, e, :], banks[3 + e // 4][:, (e % 4) * P:(e % 4) * P + P], ACT.Copy,
                                     scale=cnt[:, e:e + 1]).then_inc(ewT_ok, 1)
            attention_scalar(0)

            with act.Fori(0, B) as b:
                act.wait_ge(ct_ps, b + 1)
                nc.scalar.activation(av_s[:, :], m0[:, :], ACT.Copy).then_inc(ctT_ok, 1)
                act.wait_ge(op_ps, b + 1)
                nc.scalar.activation(qk_f[:, 0, :], banks[6][:, :], ACT.Identity, bias=bsum[:, :]).then_inc(acc0_ok, 1)

            norm_scalar(1)
            act.wait_ge(g_sub, 1)
            nc.scalar.activation(gt[:, 1, :, :], gt[:, 1, :, :], ACT.Exp).then_inc(g_exp, 1)
            attention_scalar(1)

            with act.Fori(0, (E + 1) * B // 2) as t2:
                for half in range(2):
                    for c in range(FC):
                        act.wait_ge(up_ps, FC * (2 * t2 + half) + c + 1)
                        nc.scalar.activation(hidden[half][:, c, :], banks[c][:, :], ACT.Gelu).then_inc(hid_ok, 1)

        @block.vector
        def _(dve):
            chain = Chain(dve, ch["vector"])
            link = chain.link
            vec = nc.vector

            def normalise(l):
                chain.start(chain.base + chain.k)
                with dve.Fori(0, NT) as t:
                    vec.bn_stats(stats[:, t, :], x[:, t, :]).then_inc(ch["vector"], 1)
                chain.k += NT
                dve.wait_ge(ch["vector"], chain.base + chain.k)
                me, qe, mo, qo = (stats[:, :, i] for i in (1, 2, 4, 5))
                mean, dif, var, std = lnw[:, 0, :], lnw[:, 1, :], lnw[:, 3, :], lnw[:, 4, :]
                link(vec.tensor_tensor(mean, me, mo, ALU.add))
                link(vec.tensor_scalar(mean, mean, 0.5, None, ALU.mult))
                link(vec.tensor_tensor(dif, me, mo, ALU.subtract))
                link(vec.tensor_tensor(dif, dif, dif, ALU.mult))
                link(vec.tensor_tensor(var, qe, qo, ALU.add))
                link(vec.tensor_scalar(var, var, 1.0 / D, EPS, ALU.mult, ALU.add))
                vec.scalar_tensor_tensor(var, dif, 0.25, var, ALU.mult, ALU.add).then_inc(var_ok[l], 1)
                dve.wait_ge(std_ok[l], 1)
                link(vec.reciprocal(lnw[:, 2, :], std))

                def body(b, first):
                    if l == 1 and not first:
                        dve.wait_ge(xadd_ok, b)
                    for i in range(2):
                        if not first:
                            dve.wait_ge(tr_ok[l], 2 * b + i - 1)
                        for j in range(2):
                            t = 4 * b + 2 * i + j
                            last = vec.tensor_scalar(xn[:, 2 * i + j, :], x[:, t, :], lnw[:, 0, bass.ds(t, 1)],
                                                     lnw[:, 2, bass.ds(t, 1)], ALU.subtract, ALU.mult)
                        last.then_inc(xn_ok[l], 1)
                    if l == 1:
                        dve.wait_ge(xn_ok[l], 2 * b + 2)
                        dst = x[:, bass.ds(4 * b, 4), :]
                        vec.tensor_tensor(dst, dst, xn[:, :, :], ALU.add).then_inc(xadd_ok, 1)
                    for i in range(2):
                        dve.wait_ge(xts_ok[l], 2 * b + i + 1)
                        vec.tensor_copy(xnT[:, bass.ds(b * S + i * 2 * P, 2 * P)],
                                        xts[:, 2 * i:2 * i + 2, :].rearrange("p t d -> p (t d)")
                                        ).then_inc(xnT_ok[l], 1)

                body(0, True)
                with dve.Fori(1, B) as b:
                    body(b, False)

            def top2(work):
                g, tmp, hot, hot2 = gt[:, work, :, :], gt[:, 3, :, :], gt[:, 2, :, :], gt[:, 3, :, :]
                best, at = gs[:, 2, :], gs[:, 3, :]
                wide = lambda v: v.unsqueeze(2).broadcast_to((P, NT, E))
                idx = eidx[:, :].unsqueeze(1).broadcast_to((P, NT, E))

                def onehot(src, dst):
                    link(vec.reduce_max(best, src, AX.X))
                    link(vec.tensor_tensor(tmp, src, wide(best), ALU.is_equal))
                    link(vec.tensor_tensor(tmp, tmp, idx, ALU.mult))
                    link(vec.tensor_reduce(at, tmp, AX.X, ALU.min))
                    link(vec.tensor_tensor(dst, idx, wide(at), ALU.is_equal))

                onehot(g, hot)
                rest = gt[:, 1 - work, :, :]
                link(vec.scalar_tensor_tensor(rest, hot, -3.0e38, g, ALU.mult, ALU.add))
                onehot(rest, hot2)
                return g, hot, hot2

            def attention_vector(l, base):
                a = A[l]
                lag = LAG[l]

                def prepare(b, what):
                    t = 0 if what[0] == "q" else 1
                    if what in ("q_res", "k_res"):
                        dve.wait_ge(a["hi_ok"], 2 * b + t + 1)
                        vec.tensor_tensor(qk_r[:, t, :], qk_f[:, t, :], parts[:, 3 * t, :], ALU.subtract
                                          ).then_inc(a["res_ok"], 1)
                    elif what in ("q_lo", "k_lo"):
                        dve.wait_ge(a["mid_ok"], 2 * b + t + 1)
                        vec.tensor_tensor(parts[:, 3 * t + 2, :], qk_r[:, t, :], parts[:, 3 * t + 1, :], ALU.subtract
                                          ).then_inc(a["lo_ok"], 1)
                    elif what == "v":
                        dve.wait_ge(a["v_ps"], b + 1)
                        bias = bv[:, l, :].unsqueeze(1).broadcast_to((P, KB, D))
                        vec.tensor_tensor(vtok[:, :, :, :].rearrange("p k h d -> p k (h d)"),
                                          m0[:, :].rearrange("p (k n) -> p k n", k=KB), bias, ALU.add
                                          ).then_inc(a["v_ok"], 1)
                    elif what == "gate":
                        dve.wait_ge(a["ze_ok"], b + 1)
                        link(vec.tensor_scalar(zc[:, 0, :], zc[:, 0, :], 1.0, None, ALU.add))
                        link(vec.reciprocal(zc[:, 1, :], zc[:, 0, :]))
                        link(vec.tensor_scalar(zc[:, 2, :], zc[:, 1, :], -1.0, None, ALU.add))
                        vec.tensor_tensor(zc[:, 3, :], zc[:, 2, :], zc[:, 2, :], ALU.mult)
                        vec.tensor_tensor(zc[:, 4, :], zc[:, 1, :], zc[:, 1, :], ALU.mult)
                        vec.tensor_scalar(zc[:, 5, :], zc[:, 1, :], -1.0, None, ALU.mult).then_inc(a["zc_ok"], 1)
                    elif what[:-1] == "sum":
                        i = int(what[-1])
                        dve.wait_ge(a["penx_ok"], KB * b + i + 1)
                        link(vec.scalar_tensor_tensor(pw[:, 0, :], pw[:, 0, :], zc[:, 1, i:i + 1], pw[:, 1, :],
                                                      ALU.add, ALU.subtract))
                    elif what[:-1] == "product":
                        i = int(what[-1])
                        n = KB * b + i
                        if not (isinstance(b, int) and n == 0):
                            dve.wait_ge(a["pent_ps"], n)
                        vec.scalar_tensor_tensor(pw[:, 3, :], pw[:, 2, :], 1.0, pw[:, 0, :], ALU.min, ALU.mult
                                                 ).then_inc(a["penq_ok"], 1)
                    elif what[:-1] == "put":
                        kb = int(what[-1])
                        if kb == 0:
                            dve.wait_ge(a["penraw_ok"], KB * b + KB)
                        if not (isinstance(b, int) and b == 0):
                            dve.wait_ge(a["pen_p"], N_POOL * (NG * b - 1)
                                        + sum(w not in ON_DVE for w in range(HG * (kb + 1))))
                        vec.tensor_scalar(penalty[:, kb, :], penalty_raw[:, kb, :], 1e-32, None, ALU.max
                                          ).then_inc(a["pen_ok"], 1)

                def maxima(n, G, g, u):
                    j, qb = unit_query(u)
                    width = (qb + 1) * P if l == 0 else S
                    dve.wait_ge(a["mx_ps"], n + 1)
                    vec.reduce_max(mx[:, g, u:u + 1], max_bank(g, u)[:, 0:width], AX.X).then_inc(a["mx_ok"], 1)

                def shift_mid(G, g):
                    dve.wait_ge(a["mhi_ok"], G + 1)
                    vec.scalar_tensor_tensor(mrow[:, g, 1, :], m0[0:UN, 0:P], -1.0, mrow[:, g, 0, :],
                                             ALU.mult, ALU.subtract).then_inc(a["mrow_ok"], 1)

                def tail(G, g):
                    dve.wait_ge(a["avt_ps"], G)
                    ps = m0[:, :].rearrange("p (q j c) -> p q j c", q=KB, j=HG)
                    link(vec.reciprocal(rec[:, :, :], ps[:, :, :, HD]))
                    ratio = rec[:, :, :].unsqueeze(3).broadcast_to((P, KB, HG, HD))
                    bt = (G - 1) // NG if isinstance(G, int) else None
                    return ps, ratio

                def tail_to(G, g, bt):
                    ps, ratio = tail(G, g)
                    cols = slice(g * HG * HD, (g + 1) * HG * HD)
                    if l == 0:
                        dst = context[:, bass.ds(bt * KB, KB), cols].rearrange("p q (j d) -> p q j d", j=HG)
                        vec.tensor_tensor(dst, ps[:, :, :, 0:HD], ratio, ALU.mult).then_inc(a["norm_ok"], 1)
                    else:
                        link(vec.tensor_tensor(ctx_t[:, :, :, :], ps[:, :, :, 0:HD], ratio, ALU.mult))
                        dst = x[:, bass.ds(bt * KB, KB), cols]
                        vec.tensor_tensor(dst, dst, ctx_t[:, :, :, :].rearrange("p q j d -> p q (j d)"), ALU.add
                                          ).then_inc(a["norm_ok"], 1)

                for what in ("q_res", "k_res", "q_lo", "k_lo", "v"):
                    prepare(0, what)
                if l == 1:
                    prepare(0, "gate")
                for G in range(2):
                    for u in range(UN):
                        maxima(UN * G + u, G, G, u)
                        if l == 1 and u % 8 == 7:
                            i = (UN * G + u) // 8
                            prepare(0, f"sum{i}")
                            prepare(0, f"product{i}")
                if l == 1:
                    for kb in range(KB):
                        prepare(0, f"put{kb}")
                shift_mid(0, 0)
                start = chain.base + chain.k
                per = NG if l == 0 else 2 * NG + 3 + KB

                def body(b, first, last):
                    chain.start(start + per * b)
                    for g in range(NG):
                        G = 4 * b + g
                        for u in range(UN):
                            if not (last and g >= 2):
                                if u == 0 and not (first and g < 2):
                                    dve.wait_ge(a["mt_ps"], G - 1)
                                maxima(UN * (G + 2) + u, G + 2, (g + 2) % NG, u)
                            if l == 1:
                                v = u - 1
                                if v in ON_DVE:
                                    dve.wait_ge(a["exp_ok"], UN * G + v + 1)
                                    t = probs[:, n_slot(v), :]
                                    vec.tensor_tensor(t, t, penalty[:, unit_key(v)[0], :], ALU.mult
                                                      ).then_inc(a["pen_v"], 1)
                            if l == 1 and g == 0 and 0 < u < KB and not first:
                                prepare(b, f"put{u}")
                            if u == 5 and not (last and g == NG - 1):
                                shift_mid(G + 1, (g + 1) % NG)
                            if u == lag + 5 and not (first and g == 0):
                                tail_to(G, (g - 1) % NG, b if g else b - 1)
                            if last:
                                continue
                            what = VECTOR_NEXT[l].get((g, u))
                            if what == "v":
                                dve.wait_ge(a["vexp_ok"], NG * b + NG)
                            if what:
                                prepare(b + 1, what)
                    chain.fill(per)

                over_batches(dve, body)
                chain.start(start + per * B)
                tail_to(B * NG, NG - 1, B - 1)

            dve.wait_ge(consts, 12)
            vec.tensor_copy(eidx[:, :], eidx_i[:, :]).then_inc(consts, 1)
            link(vec.tensor_copy(dist[:, :], disti[:, :]))
            link(vec.scalar_tensor_tensor(dist[:, :], dist[:, :], -1.0, dist[:, :], ALU.mult, ALU.max))
            vec.tensor_scalar(dist[:, :], dist[:, :], -1.0, 2.0, ALU.mult, ALU.add).then_inc(consts, 1)
            dve.wait_ge(d_w, 16 * LOADS)
            for l in (0, 1):
                for t in range(2):
                    vec.tensor_copy(wproj[:, l, t, :].rearrange("p (d h) -> p d h", d=HD),
                                    wraw[:, l, t, :].rearrange("p (h d) -> p d h", d=HD)).then_inc(wready, 1)
                vec.tensor_copy(wproj[:, l, 2, :], wraw[:, l, 2, :]).then_inc(wready, 1)
                vec.tensor_scalar(bqk[:, l, 1:2], bqk[:, l, 1:2], HD ** -0.5, None, ALU.mult).then_inc(wready, 1)
            vec.tensor_scalar(nbg[:, :], bg[:, :], -1.0, None, ALU.mult).then_inc(wready, 1)

            dve.wait_ge(d_x, 64)
            normalise(0)
            dve.wait_ge(logits_ok[0], NT)
            gb = bgate[:, :].unsqueeze(1).broadcast_to((P, NT, E))
            dve.wait_ge(consts, 14)
            link(vec.tensor_tensor(gt[:, 0, :, :], banks[2][:, 0:NT * E].rearrange("p (t e) -> p t e", e=E), gb, ALU.add))
            g, hot, hot2 = top2(0)
            vec.tensor_tensor(gt[:, 0, :, :], hot, hot2, ALU.add).then_inc(mask_ok, 1)
            dve.wait_ge(cnt_ps, 1)
            link(vec.reduce_sum(cnt[:, :], banks[2][:, 0:NT * E].rearrange("p (t e) -> p e t", e=E), AX.X))
            link(vec.tensor_scalar(cnt[:, :], cnt[:, :], 1.0 / (2 * TOKENS), None, ALU.mult))
            link(vec.scalar_tensor_tensor(nb[:, :], cnt[:, :], -1.0, eb[:, :], ALU.mult, ALU.mult))
            link(vec.reduce_sum(bsum[:, :], nb[:, :], AX.X))
            vec.tensor_tensor(bsum[:, :], bo[:, :], bsum[:, :], ALU.subtract).then_inc(cnt_ok, 1)

            attention_vector(0, 0)

            start = chain.base + chain.k
            dve.wait_ge(A[0]["norm_ok"], B * NG)

            def out_body(b, first):
                chain.start(start + E * b)
                if not first:
                    dve.wait_ge(ct_ps, b)
                vec.tensor_copy(xts[:, :, :], context[:, bass.ds(b * KB, KB), :]).then_inc(ctile_ok, 1)
                dve.wait_ge(acc0_ok, b + 1)
                acc = qk_f[:, 0, :]
                for e in range(E):
                    dve.wait_ge(ff_ps, E * b + e + 1)
                    ins = vec.scalar_tensor_tensor(acc, banks[e % 4][:, :], nb[:, e:e + 1], acc, ALU.max, ALU.add)
                    ins.then_inc(acc_ok, 1)
                    dve.wait_ge(acc_ok, E * b + e + 1)
                dve.wait_ge(yT_ps, b + 1)
                dst = x[:, bass.ds(b * KB, KB), :]
                vec.tensor_tensor(dst, dst, banks[4][:, :].rearrange("p (t d) -> p t d", t=KB), ALU.add
                                  ).then_inc(x1_ok, 1)

            out_body(0, True)
            with dve.Fori(1, B) as b:
                out_body(b, False)
            chain.start(start)
            dve.wait_ge(x1_ok, B)

            normalise(1)
            dve.wait_ge(logits_ok[1], NT)
            wide = lambda v: v.unsqueeze(2).broadcast_to((P, NT, E))
            lg = banks[2][:, 0:NT * E].rearrange("p (t e) -> p t e", e=E)
            link(vec.reduce_max(gs[:, 0, :], lg, AX.X))
            vec.tensor_tensor(gt[:, 1, :, :], lg, wide(gs[:, 0, :]), ALU.subtract).then_inc(g_sub, 1)
            dve.wait_ge(g_exp, 1)
            link(vec.reduce_sum(gs[:, 0, :], gt[:, 1, :, :], AX.X))
            link(vec.reciprocal(gs[:, 1, :], gs[:, 0, :]))
            link(vec.tensor_tensor(gt[:, 1, :, :], gt[:, 1, :, :], wide(gs[:, 1, :]), ALU.mult))
            g, hot, hot2 = top2(1)
            link(vec.tensor_tensor(hot, hot, hot2, ALU.add))
            link(vec.tensor_tensor(gt[:, 2, :, :], hot, g, ALU.mult))

            attention_vector(1, 0)
            dve.wait_ge(A[1]["norm_ok"], B * NG)

            dve.sem_inc(add_ok, 2)
            def expert_add(e, n0):
                def one(b, half):
                    n = n0 + 2 * b + half
                    dve.wait_ge(dn_ps, n + 1)
                    for i in range(KB):
                        t = KB * (2 * b + half) + i
                        src = banks[4 + half][:, i * P:(i + 1) * P]
                        gate = 1.0 if e == 0 else gt[:, 2, t, e - 1:e]
                        ins = vec.scalar_tensor_tensor(x[:, t, :], src, gate, x[:, t, :], ALU.mult, ALU.add)
                    ins.then_inc(add_ok, 1)

                with dve.Fori(0, B // 2) as b:
                    for half in range(2):
                        one(b, half)
                dve.wait_ge(add_ok, 2 + n0 + B)

            for e in range(E + 1):
                expert_add(e, B * e)

        @block.tensor
        def _(pe):
            mm = nc.tensor.matmul
            transpose = nc.tensor.transpose

            def normalise(l):
                def body(b, first):
                    for i in range(2):
                        pe.wait_ge(xn_ok[l], 2 * b + i + 1)
                        if not first:
                            pe.wait_ge(xts_ok[l], 2 * b + i - 1)
                        for j in range(2):
                            last = transpose(banks[i][:, j * P:(j + 1) * P], xn[:, 2 * i + j, :], ident[:, :])
                        last.then_inc(tr_ok[l], 1)
                    for i in range(2):
                        pe.wait_ge(xts_ok[l], 2 * b + i + 1)
                        for j in range(2):
                            mm(banks[2][:, bass.ds((4 * b + 2 * i + j) * E, E)], xts[:, 2 * i + j, :], wgate[:, l, :],
                               start=True, stop=True).then_inc(logits_ok[l], 1)

                if l == 0:
                    pe.wait_ge(consts, 14)
                    pe.wait_ge(d_w, 16 * LOADS)
                body(0, True)
                with pe.Fori(1, B) as b:
                    body(b, False)

            def attention_tensor(l):
                a = A[l]
                lag = LAG[l]

                spare_last = [None]

                def spare(what, b):
                    if spare_last[0] is not None:
                        pe.wait_ge(*spare_last[0])
                    if what == "q":
                        pe.wait_ge(a["xb_ok"], b + 1)
                    if what in ("q", "k"):
                        t = 0 if what == "q" else 1
                        mm(m0[:, :], wproj[:, l, t, :], xb[:, :], start=True, stop=True).then_inc(a["qk_ps"], 1)
                        spare_last[0] = (a[what + "_used"], b + 1)
                    elif what == "v":
                        for kb in range(KB):
                            last = mm(m0[:, kb * P:(kb + 1) * P], xb[:, kb * P:(kb + 1) * P], wproj[:, l, 2, :],
                                      start=True, stop=True)
                        last.then_inc(a["v_ps"], 1)
                        spare_last[0] = (a["v_ok"], b + 1)
                    elif what == "gate":
                        for kb in range(KB):
                            last = mm(m0[:, kb:kb + 1], xb[:, kb * P:(kb + 1) * P], wg[:, :], start=True, stop=True)
                        last.then_inc(a["zc_ps"], 1)
                        spare_last[0] = (a["ze_ok"], b + 1)
                    elif what == "gates":
                        pe.wait_ge(a["zc_ok"], b + 1)
                        for kb in range(KB):
                            last = mm(m0[:, kb * P:(kb + 1) * P], zc[:, 1, kb:kb + 1].broadcast_to((P, P)),
                                      ident[:, :], start=True, stop=True)
                        last.then_inc(a["zr_ps"], 1)
                        spare_last[0] = (a["zr_ok"], b + 1)
                    elif what.startswith("penalty"):
                        i = int(what[-1])
                        pe.wait_ge(a["penq_ok"], KB * b + i + 1)
                        for kb in range(KB):
                            last = transpose(m0[:, kb * P:(kb + 1) * P], pw[:, 3, kb * P:(kb + 1) * P], ident[:, :])
                        last.then_inc(a["pent_ps"], 1)
                        spare_last[0] = (a["penraw_ok"], KB * b + i + 1)

                def turn_maxima(G, g):
                    if spare_last[0] is not None:
                        pe.wait_ge(*spare_last[0])
                    pe.wait_ge(a["mx_ok"], UN * (G + 1))
                    transpose(m0[0:UN, 0:P], mx[:, g, :], ident[:, :]).then_inc(a["mt_ps"], 1)
                    spare_last[0] = (a["mrow_ok"], G + 1)

                def turn_context(G):
                    if spare_last[0] is not None:
                        pe.wait_ge(*spare_last[0])
                    pe.wait_ge(a["av_s_ok"], G)
                    for qb in range(KB):
                        last = transpose(m0[:, qb * P:(qb + 1) * P], av_s[:, qb * P:(qb + 1) * P], ident[:, :])
                    last.then_inc(a["avt_ps"], 1)
                    spare_last[0] = (a["norm_ok"], G)

                def score_max(n, g, u, free):
                    j, qb = unit_query(u)
                    bank = max_bank(g, u)
                    if free is not None:
                        pe.wait_ge(a["mx_ok"], free)
                    lhs = qst[0:SHIFT_ROW, g, j * S + qb * P:j * S + (qb + 1) * P]
                    if l == 0:
                        mm(bank[:, 0:(qb + 1) * P], lhs, kst[0:SHIFT_ROW, g, j * S:j * S + (qb + 1) * P],
                           start=True, stop=False)
                        mm(bank[:, qb * P:(qb + 1) * P], ident16[:, :], mask_q[:, :], start=False, stop=True
                           ).then_inc(a["mx_ps"], 1)
                    else:
                        mm(bank[:, :], lhs, kst[0:SHIFT_ROW, g, j * S:(j + 1) * S], start=True, stop=True
                           ).then_inc(a["mx_ps"], 1)

                def score(n, g, u, free):
                    kb, j = unit_key(u)
                    bank = scb[u % 2]
                    if free is not None:
                        pe.wait_ge(a["exp_ok"], free)
                    rows = slice(0, SHIFT_ROW + 2)
                    lhs = kst[rows, g, j * S + kb * P:j * S + (kb + 1) * P]
                    if l == 0:
                        mm(bank[:, 0:S - kb * P], lhs, qst[rows, g, j * S + kb * P:(j + 1) * S], start=True, stop=False)
                        mm(bank[:, 0:P], ident16[:, :], mask_k[:, :], start=False, stop=True).then_inc(a["sc_ps"], 1)
                    else:
                        mm(bank[:, :], lhs, qst[rows, g, j * S:(j + 1) * S], start=True, stop=True).then_inc(a["sc_ps"], 1)

                def weigh(n, G, g, u):
                    kb, j = unit_key(u)
                    if l == 0:
                        pe.wait_ge(a["exp_ok"], n + 1)
                    elif u in ON_DVE:
                        pe.wait_ge(a["pen_v"], len(ON_DVE) * G + sum(v <= u for v in ON_DVE))
                    else:
                        pe.wait_ge(a["pen_p"], (UN - len(ON_DVE)) * G + sum(v <= u for v in range(UN) if v not in ON_DVE))
                    lo = kb * P if l == 0 else 0
                    last = mm(avb[g % 2][32 * j:32 * j + 32, lo:S], vexp[:, g, kb, j, :], probs[:, n_slot(u), lo:S],
                              start=(kb == 0), stop=(kb == KB - 1))
                    last.then_inc(a["av_ps"], 1)

                pe.wait_ge(wready, 9)
                pe.wait_ge(xnT_ok[l], 2 * B)
                for what in ("q", "k", "v"):
                    spare(what, 0)
                if l == 1:
                    spare("gate", 0)
                    spare("gates", 0)
                for G in range(2):
                    pe.wait_ge(a[f"stacked{G}"], 6 * 16)
                    for u in range(UN):
                        n = UN * G + u
                        score_max(n, G, u, n - max_bank_last(G, u) + 1 if n >= 3 else None)
                        if l == 1 and n % 8 == 3 and n > 8:
                            spare(f"penalty{n // 8 - 1}", 0)
                if l == 1:
                    spare(f"penalty{KB - 1}", 0)
                turn_maxima(0, 0)

                def body(b, first, last):
                    if not first:
                        spare_last[0] = (a["norm_ok"], NG * b - 1) if l == 0 else (a["penraw_ok"], KB * (b + 1))
                    for g in range(NG):
                        G = 4 * b + g
                        for u in range(UN):
                            if not (last and g >= 2):
                                g2, n2 = (g + 2) % NG, UN * (G + 2) + u
                                if u == 0:
                                    pe.wait_ge(a[f"stacked{g2}"], 6 * 16 * ((b if g < 2 else b + 1) + 1))
                                score_max(n2, g2, u, n2 - max_bank_last(g2, u) + 1)
                            if u == 0:
                                pe.wait_ge(a[f"shift{g}"], 32 * (b + 1))
                            n = UN * G + u
                            score(n, g, u, None if first and g == 0 and u < 2 else n - 1)
                            if u >= lag:
                                if u == lag and not (first and g < 1):
                                    if not (first and g < 2):
                                        pe.wait_ge(a["av_s_ok"], G - 1)
                                if u == lag:
                                    pe.wait_ge(a["vexp_ok"], vexp_needed(b, g, first))
                                weigh(n - lag, G, g, u - lag)
                            elif not (first and g == 0):
                                weigh(n - lag, G - 1, (g - 1) % NG, UN + u - lag)
                            every = SPARE[l]["every"].get(u)
                            if every == "maxima" and not (last and g == NG - 1):
                                turn_maxima(G + 1, (g + 1) % NG)
                            if every == "contexts" and not (first and g == 0):
                                turn_context(G)
                            if (g, u) in SPARE[l]["next"] and not last:
                                spare(SPARE[l]["next"][g, u], b + 1)

                def vexp_needed(b, g, first):
                    return NG if first else NG * b + g + 1

                over_batches(pe, body)
                for u in range(UN - lag, UN):
                    weigh(UN * (NG * B - 1) + u, NG * B - 1, NG - 1, u)
                turn_context(NG * B)

            normalise(0)
            for e in range(E):
                last = transpose(banks[3 + e // 4][:, (e % 4) * P:(e % 4) * P + P], ew[:, e, :], ident[:, :])
                if e % 4 == 3:
                    last.then_inc(ewT_ps, 1)
            pe.wait_ge(mask_ok, 1)
            mm(banks[2][:, 0:NT * E], ones[:, :], gt[:, 0, :, :].rearrange("p t e -> p (t e)"),
               start=True, stop=True).then_inc(cnt_ps, 1)
            pe.wait_ge(cnt_ok, 1)
            pe.wait_ge(ewT_ok, E)
            attention_tensor(0)

            def out_body(b, first):
                pe.wait_ge(ctile_ok, b + 1)
                if not first:
                    pe.wait_ge(ctT_ok, b)
                else:
                    pe.wait_ge(A[0]["norm_ok"], B * NG)
                for i in range(KB):
                    last = transpose(m0[:, i * P:(i + 1) * P], xts[:, i, :], ident[:, :])
                last.then_inc(ct_ps, 1)
                pe.wait_ge(ctT_ok, b + 1)
                if not first:
                    pe.wait_ge(acc0_ok, b)
                mm(banks[6][:, :], wout[:, :], av_s[:, :], start=True, stop=True).then_inc(op_ps, 1)
                for e in range(E):
                    if not (first and e < 4):
                        pe.wait_ge(acc_ok, E * b + e - 3)
                    mm(banks[e % 4][:, :], ewT[:, e, :], xnT[:, bass.ds(b * S, S)], start=True, stop=True
                       ).then_inc(ff_ps, 1)
                pe.wait_ge(acc_ok, E * b + E)
                if not first:
                    pe.wait_ge(x1_ok, b)
                for i in range(KB):
                    last = transpose(banks[4][:, i * P:(i + 1) * P], qk_f[:, 0, i * P:(i + 1) * P], ident[:, :])
                last.then_inc(yT_ps, 1)

            out_body(0, True)
            with pe.Fori(1, B) as b:
                out_body(b, False)
            normalise(1)
            attention_tensor(1)

            def expert_half(e, n, tb, half, first):
                for c in range(FC):
                    if not first:
                        pe.wait_ge(hid_ok, FC * (n - 1) + c + 1)
                    mm(banks[c][:, :], w_up[e % 2][:, c * P:(c + 1) * P], xnT[:, bass.ds(tb * S, S)],
                       start=True, stop=True).then_inc(up_ps, 1)

            def down(e, n, half):
                pe.wait_ge(hid_ok, FC * n + FC)
                pe.wait_ge(add_ok, n + 1)
                for i in range(KB):
                    for c in range(FC):
                        last = mm(banks[4 + half][:, i * P:(i + 1) * P], hidden[half][:, c, i * P:(i + 1) * P],
                                  w_dn[e % 2][:, c, :], start=(c == 0), stop=(c == FC - 1))
                last.then_inc(dn_ps, 1)

            pe.wait_ge(A[1]["norm_ok"], B * NG)
            for e in range(E + 1):
                pe.wait_ge(w_in[e % 2], 32 * (e // 2 + 1))
                expert_half(e, B * e, 0, 0, e == 0)
                with pe.Fori(0, B // 2 - 1) as t:
                    n = B * e + 2 * t
                    expert_half(e, n + 1, 2 * t + 1, 1, False)
                    down(e, n, 0)
                    expert_half(e, n + 2, 2 * t + 2, 0, False)
                    down(e, n + 1, 1)
                n = B * e + B - 2
                expert_half(e, n + 1, B - 1, 1, False)
                down(e, n, 0)
                down(e, n + 1, 1)

    return nc


_ARGS = {
    "x": "L0_attn_x", "Wqkv": "L0_attn_Wqkv", "bqkv": "L0_attn_bqkv", "Wout": "L0_attn_Wout", "bout": "L0_attn_bout",
    "gate_w": "L0_ffn_gate_w", "gate_b": "L0_ffn_gate_b", "expert_w": "L0_ffn_expert_w", "expert_b": "L0_ffn_expert_b",
    "Wq": "L1_attn_Wq", "bq": "L1_attn_bq", "Wk": "L1_attn_Wk", "bk": "L1_attn_bk", "Wv": "L1_attn_Wv", "bv": "L1_attn_bv",
    "Wg": "L1_attn_Wg", "bg": "L1_attn_bg", "shared_up": "L1_ffn_shared_up", "shared_down": "L1_ffn_shared_down",
    "routed_up": "L1_ffn_routed_up", "routed_down": "L1_ffn_routed_down", "router_w": "L1_ffn_router_w",
}


def kernel(**inputs):
    import concourse.bacc as bacc
    from concourse.bass_utils import run_bass_kernel_spmd

    nc = bacc.Bacc("TRN2", target_bir_lowering=False, num_devices=1)
    arrays, io = {}, {}
    for short, name in _ARGS.items():
        a = np.ascontiguousarray(inputs[name])
        arrays["in_" + short] = a
        io[short] = nc.dram_tensor("in_" + short, a.shape, mybir.dt.from_np(a.dtype), kind="ExternalInput").ap()
    out = nc.dram_tensor("out", (B, S, D), F32, kind="ExternalOutput").ap()
    program(nc, io, out)
    r = run_bass_kernel_spmd(nc, [arrays], core_ids=[0])
    return r.results[0]["out"]
```

```python
from contextlib import ExitStack

import numpy as np

import concourse.bass as bass
from concourse import mybir

ALU = mybir.AluOpType
ACT = mybir.ActivationFunctionType
AX = mybir.AxisListType
F32 = mybir.dt.float32
BF16 = mybir.dt.bfloat16
F16 = mybir.dt.float16

P = 128
B, S, D = 8, 512, 128
NH, HD = 16, 8
NT = B * S // P
KB = S // P
NG, HG = 4, 4
UN = KB * HG
E = 8
F = 512
FC = F // P
EPS = 1e-5
KROWS = 72
SHIFT_ROW = 96
PRING = 8
LAG = (3, 6)
TOKENS = B * S
W_SCALE, H_SCALE = 64.0, 16.0
LOADS = 15 + 4 * HD
ON_DVE = (2, 6, 10, 14)

N_POOL = UN - len(ON_DVE)

SPARE = (
    {"every": {2: "maxima", 7: "contexts"},
     "next": {(0, 10): "q", (0, 12): "k", (0, 14): "v"}},
    {"every": {2: "maxima", 10: "contexts"},
     "next": {(0, 7): "q", (0, 13): "k", (0, 15): "v", (1, 7): "gate", (1, 13): "gates",
              (2, 7): "penalty0", (2, 13): "penalty1", (3, 7): "penalty2", (3, 13): "penalty3"}},
)
SCALAR_NEXT = (
    {(0, 5): "xb", (0, 11): "q", (0, 12): "q_hi", (0, 13): "k", (0, 14): "k_hi", (0, 15): "q_mid", (1, 0): "k_mid"},
    {(0, 5): "xb", (0, 8): "q", (0, 9): "q_hi", (0, 13): "q_mid", (0, 14): "k", (0, 15): "k_hi", (1, 2): "k_mid",
     (1, 8): "gate", (1, 12): "reach", (1, 14): "gates",
     (1, 15): "u0", (2, 0): "t0", (2, 1): "s0", (2, 8): "raw0", (2, 5): "u1", (2, 6): "t1", (2, 7): "s1", (2, 14): "raw1",
     (2, 12): "u2", (2, 13): "t2", (2, 15): "s2", (3, 8): "raw2", (3, 2): "u3", (3, 3): "t3", (3, 5): "s3",
     (3, 14): "raw3"},
)
VECTOR_NEXT = (
    {(0, 13): "q_res", (0, 15): "k_res", (1, 0): "v", (1, 1): "q_lo", (1, 2): "k_lo"},
    {(0, 12): "q_res", (0, 14): "q_lo", (1, 0): "v", (1, 1): "k_res", (1, 4): "k_lo", (1, 10): "gate",
     (2, 2): "sum0", (2, 3): "product0", (2, 9): "sum1", (2, 10): "product1",
     (3, 0): "sum2", (3, 1): "product2", (3, 8): "sum3", (3, 9): "product3", (3, 15): "put0"},
)


class Chain:

    def __init__(self, eng, sem):
        self.eng, self.sem, self.base, self.k = eng, sem, 0, 0

    def link(self, ins):
        self.k += 1
        ins.then_inc(self.sem, 1)
        self.eng.wait_ge(self.sem, self.base + self.k)

    def start(self, base):
        self.base, self.k = base, 0

    def fill(self, per):
        assert self.k <= per, self.k
        if self.k < per:
            self.eng.sem_inc(self.sem, per - self.k)


def program(nc, io, out):
    ctx = ExitStack()
    with ctx:
        def sb(name, shape, dt=F32):
            return ctx.enter_context(nc.sbuf_tensor(name, shape, dt))

        def sem(name):
            return ctx.enter_context(nc.semaphore(name))

        x = sb("x", [P, NT, D])
        xnT = sb("xnT", [P, TOKENS])
        big = sb("big", [P, 16 * S])
        context = big[:, 0:NT * D].rearrange("p (t d) -> p t d", t=NT)
        penalty = big[:, 0:KB * S].rearrange("p (k q) -> p k q", k=KB)
        penalty_raw = big[:, KB * S:2 * KB * S].rearrange("p (k q) -> p k q", k=KB)
        qst = sb("qst", [P, NG, HG * S], BF16)
        kst = sb("kst", [P, NG, HG * S], BF16)
        probs = sb("probs", [P, PRING, S])
        parts = sb("parts", [P, 6, S], BF16)
        qk_f = sb("qk_f", [P, 2, S])
        qk_r = sb("qk_r", [P, 2, S])
        vexp = sb("vexp", [P, NG, KB, HG, 32])
        vtok = sb("vtok", [P, KB, NH, HD])
        xb = sb("xb", [P, S])
        av_s = sb("av_s", [P, S])
        mx = sb("mx", [P, NG, UN])
        mrow = sb("mrow", [UN, NG, 2, P], BF16)
        wproj = sb("wproj", [P, 2, 3, D])
        wraw = big[:, 6144:6144 + 2 * 3 * D].rearrange("p (l t n) -> p l t n", l=2, t=3)
        wout = sb("wout", [P, D])
        bqk = sb("bqk", [P, 2, 2])
        bv = sb("bv", [P, 2, D])
        bo = sb("bo", [P, 1])
        ident = sb("ident", [P, P])
        ident16 = sb("ident16", [P, P], F16)
        mask_q = sb("mask_q", [P, P], F16)
        mask_k = sb("mask_k", [P, P], F16)
        ones = sb("ones", [P, P])
        dist = sb("dist", [P, 2 * S - P])
        disti = big[:, 7168:7168 + 2 * S - P].bitcast(mybir.dt.int32)
        w_raw = sb("w_raw", [P, 2, 2, F])
        stats = sb("stats", [P, NT, 6])
        lnw = sb("lnw", [P, 5, NT])
        xn = probs[:, :, :].rearrange("p s (t d) -> p (s t) d", t=KB)
        xts = [qk_r[:, i, :].rearrange("p (t d) -> p t d", t=KB) for i in range(2)]
        xsplit = sb("xsplit", [P, 2, TOKENS], F16)
        w_split = sb("w_split", [P, 2, 4, F], F16)
        wgate = sb("wgate", [P, 2, E])
        bgate = sb("bgate", [P, E])
        eidx = sb("eidx", [P, E])
        eidx_i = sb("eidx_i", [P, E], mybir.dt.int32)
        gt = sb("gt", [P, 4, NT, E])
        gs = sb("gs", [P, 4, NT])
        cnt = sb("cnt", [P, E])
        ew = big[:, 4096:5120].rearrange("p (e d) -> p e d", e=E)
        ewT = big[:, 5120:6144].rearrange("p (e d) -> p e d", e=E)
        eb = sb("eb", [P, E])
        nb = sb("nb", [P, E])
        bsum = sb("bsum", [P, 1])
        rec = sb("rec", [P, KB, HG])
        ctx_t = sb("ctx_t", [P, KB, HG, HD])
        wg = sb("wg", [P, 1])
        bg = sb("bg", [P, 1])
        nbg = sb("nbg", [P, 1])
        zc = sb("zc", [P, 7, KB])
        lnbase = sb("lnbase", [P, 1])
        zrow = sb("zrow", [P, S])
        pw = sb("pw", [P, 4, S])

        banks = [ctx.enter_context(nc.psum_tensor(f"bank{i}", [P, S], F32)) for i in range(8)]
        mxb, scb, avb, m0 = banks[0:3], banks[3:5], banks[5:7], banks[7]
        scratch = nc.dram_tensor("qk_parts", [6, P, S], BF16, kind="Internal")

        d_x, d_w, d_out = sem("d_x"), sem("d_w"), sem("d_out")
        consts = sem("consts")
        cleared = sem("cleared")
        wready = sem("wready")
        ch = {n: sem(f"chain_{n}") for n in ("vector", "scalar", "gpsimd")}
        var_ok = [sem(f"var_ok{l}") for l in (0, 1)]
        std_ok = [sem(f"std_ok{l}") for l in (0, 1)]
        xn_ok = [sem(f"xn_ok{l}") for l in (0, 1)]
        tr_ok = [sem(f"tr_ok{l}") for l in (0, 1)]
        xts_ok = [sem(f"xts_ok{l}") for l in (0, 1)]
        xnT_ok = [sem(f"xnT_ok{l}") for l in (0, 1)]
        logits_ok = [sem(f"logits_ok{l}") for l in (0, 1)]
        g_sub, g_exp, mask_ok, cnt_ps, cnt_ok, ewT_ps, ewT_ok = (
            sem(n) for n in ("g_sub", "g_exp", "mask_ok", "cnt_ps", "cnt_ok", "ewT_ps", "ewT_ok"))
        A = []
        for l in (0, 1):
            names = ("stacked0 stacked1 stacked2 stacked3 shift0 shift1 shift2 shift3 spilled xb_ok "
                     "qk_ps q_used k_used hi_ok res_ok mid_ok lo_ok v_ps v_ok vexp_ok "
                     "mx_ps mx_ok mt_ps mhi_ok mrow_ok reach_ok sc_ps exp_ok pen_v pen_p av_ps "
                     "av_s_ok avt_ps norm_ok zc_ps ze_ok zc_ok zr_ps zr_ok penx_ok penq_ok "
                     "pent_ps penraw_ok pen_ok").split()
            A.append({n: sem(f"{n}_{l}") for n in names})
        ctile_ok, ct_ps, ctT_ok, op_ps, acc0_ok, ff_ps, acc_ok, yT_ps, x1_ok = (
            sem(n) for n in ("ctile_ok", "ct_ps", "ctT_ok", "op_ps", "acc0_ok", "ff_ps", "acc_ok", "yT_ps", "x1_ok"))
        w_in = [sem("w_in0"), sem("w_in1")]
        w_hi_ok, w_lo_ok, x_hi_ok, x_lo_ok = (sem(n) for n in ("w_hi_ok", "w_lo_ok", "x_hi_ok", "x_lo_ok"))
        up_ps, hid_ok, h_hi_ok, h_lo_ok, dn_ps, add_ok = (
            sem(n) for n in ("up_ps", "hid_ok", "h_hi_ok", "h_lo_ok", "dn_ps", "add_ok"))

        block = ctx.enter_context(nc.Block())

        def n_slot(u):
            return u % PRING

        def max_bank(g, u):
            return mxb[(UN * g + u) % 3]

        def max_bank_last(g, u):
            i = UN * g + u
            return 3 if i >= 3 else (1, 4, 4)[i]

        def over_batches(eng, body):
            body(0, True, False)
            with eng.Fori(1, B - 1) as b:
                body(b, False, False)
            body(B - 1, False, True)

        def unit_key(u):
            return u // HG, u % HG

        def unit_query(u):
            return u // KB, u % KB

        hidden = [probs[:, i * FC:(i + 1) * FC, :] for i in range(2)]
        h_split = [big[:, i * 2048:(i + 1) * 2048].bitcast(F16).rearrange("p (s c q) -> p s c q", s=2, c=FC)
                   for i in range(2)]

        @block.sync
        def _(sp):
            for c in range(4):
                sp.dma_start(x[:, c * 8:(c + 1) * 8, :],
                             io["x"].rearrange("b s d -> (b s) d").rearrange("(t p) d -> p t d", p=P)[:, c * 8:(c + 1) * 8, :]
                             ).then_inc(d_x, 16)

            def expert_load(e):
                if e >= 2:
                    sp.wait_ge(w_lo_ok, 2 * (e - 1))
                up = io["shared_up"][0] if e == 0 else io["routed_up"][e - 1]
                dn = io["shared_down"][0] if e == 0 else io["routed_down"][e - 1]
                sp.dma_start(w_raw[:, e % 2, 0, :], up).then_inc(w_in[e % 2], 16)
                sp.dma_start(w_raw[:, e % 2, 1, :].rearrange("p (c h) -> p c h", c=FC),
                             dn.rearrange("(c p) h -> p c h", p=P)).then_inc(w_in[e % 2], 16)

            for e in range(2):
                expert_load(e)
            sp.wait_ge(cleared, 3)
            for l in (0, 1):
                a = A[l]

                def spill(b):
                    if not (isinstance(b, int) and b == 0):
                        for g in range(NG):
                            sp.wait_ge(a[f"stacked{g}"], 96 * b)
                    sp.wait_ge(a["lo_ok"], 2 * b + 2)
                    sp.dma_start(scratch.ap().rearrange("s p q -> p s q"), parts[:, :, :]).then_inc(a["spilled"], 16)
                    sp.wait_ge(a["spilled"], 16 * b + 16)

                def stack(g):
                    for so in range(3):
                        rows = slice(24 * so, 24 * so + 24)
                        q_src = bass.AP(tensor=scratch.ap().tensor, offset=so * P * S + g * HG * S,
                                        ap=[[0, 3], [NH * S, HD], [1, HG * S]])
                        k_src = bass.AP(tensor=scratch.ap().tensor, offset=3 * P * S + g * HG * S,
                                        ap=[[P * S, 3], [NH * S, HD], [1, HG * S]])
                        sp.dma_start(qst[rows, g, :], q_src).then_inc(a[f"stacked{g}"], 16)
                        sp.dma_start(kst[rows, g, :], k_src).then_inc(a[f"stacked{g}"], 16)

                def shift(G, g):
                    sp.wait_ge(a["mrow_ok"], G + 1)
                    for r in range(2):
                        sp.dma_start(qst[SHIFT_ROW + r:SHIFT_ROW + r + 1, g, :], mrow[0:UN, g, r, :]
                                     ).then_inc(a[f"shift{g}"], 16)

                spill(0)
                for g in range(NG):
                    stack(g)
                shift(0, 0)

                def body(b, first, last):
                    for g in range(NG):
                        G = 4 * b + g
                        if not (first if g == 0 else last):
                            if g == 1:
                                spill(b + 1)
                            sp.wait_ge(a["sc_ps"], UN * G)
                            stack((g - 1) % NG)
                        if not (last and g == NG - 1):
                            shift(G + 1, (g + 1) % NG)

                over_batches(sp, body)
            for e in range(2, E + 1):
                expert_load(e)
            for b in range(B):
                sp.wait_ge(add_ok, 2 + B * E + b + 1)
                sp.dma_start(out[b].rearrange("(t p) d -> p t d", p=P), x[:, 4 * b:4 * b + 4, :]).then_inc(d_out, 16)
            sp.wait_ge(d_out, 16 * B)

        @block.gpsimd
        def _(pool):
            chain = Chain(pool, ch["gpsimd"])
            link = chain.link
            link(nc.gpsimd.memset(ident[:, :], 0.0))
            nc.gpsimd.affine_select(out=ident[:, :], in_=ident[:, :], compare_op=ALU.not_equal, fill=1.0,
                                    base=0, pattern=[[-1, P]], channel_multiplier=1).then_inc(consts, 1)
            link(nc.gpsimd.memset(ident16[:, :], 0.0))
            nc.gpsimd.affine_select(out=ident16[:, :], in_=ident16[:, :], compare_op=ALU.not_equal, fill=1.0,
                                    base=0, pattern=[[-1, P]], channel_multiplier=1).then_inc(consts, 1)
            link(nc.gpsimd.memset(mask_q[:, :], 0.0))
            nc.gpsimd.affine_select(out=mask_q[:, :], in_=mask_q[:, :], compare_op=ALU.is_ge, fill=-10000.0,
                                    base=0, pattern=[[-1, P]], channel_multiplier=1).then_inc(consts, 1)
            link(nc.gpsimd.memset(mask_k[:, :], 0.0))
            nc.gpsimd.affine_select(out=mask_k[:, :], in_=mask_k[:, :], compare_op=ALU.is_ge, fill=-10000.0,
                                    base=0, pattern=[[1, P]], channel_multiplier=-1).then_inc(consts, 1)
            nc.gpsimd.memset(ones[:, :], 1.0).then_inc(consts, 1)
            nc.gpsimd.memset(lnbase[:, :], float(np.log(S - 2.0))).then_inc(consts, 1)
            nc.gpsimd.iota(eidx_i[:, :], pattern=[[1, E]], base=-E, channel_multiplier=0).then_inc(consts, 1)
            nc.gpsimd.iota(disti[:, :], pattern=[[1, 2 * S - P]], base=-(S - P), channel_multiplier=-1).then_inc(consts, 1)
            pool.wait_ge(consts, 8)
            nc.gpsimd.memset(qst[64:SHIFT_ROW, :, :], 0.0).then_inc(cleared, 1)
            pool.wait_ge(cleared, 1)
            nc.gpsimd.memset(kst[64:SHIFT_ROW, :, :], 0.0).then_inc(cleared, 1)
            pool.wait_ge(cleared, 2)
            nc.gpsimd.memset(kst[SHIFT_ROW:SHIFT_ROW + 2, :, :], 1.0).then_inc(cleared, 1)
            pool.wait_ge(cleared, 3)
            link(nc.gpsimd.memset(vexp[:, :, :, :, HD + 1:32], 0.0))
            nc.gpsimd.memset(vexp[:, :, :, :, HD:HD + 1], 1.0).then_inc(cleared, 1)

            pool.wait_ge(xnT_ok[1], B)
            nc.gpsimd.tensor_copy(xsplit[:, 0, :], xnT[:, :]).then_inc(x_hi_ok, 1)
            pool.wait_ge(x_hi_ok, 1)
            nc.gpsimd.tensor_tensor(xsplit[:, 1, :], xnT[:, :], xsplit[:, 0, :], ALU.subtract).then_inc(x_lo_ok, 1)

            a = A[1]
            in_pool = [u for u in range(UN) if u not in ON_DVE]
            def body(b, first, last):
                for g in range(NG):
                    G = 4 * b + g
                    for u in range(UN):
                        if u in in_pool:
                            kb = unit_key(u)[0]
                            n = UN * G + u
                            if g == 0:
                                pool.wait_ge(a["pen_ok"], KB * b + kb + 1)
                            pool.wait_ge(a["exp_ok"], n + 1)
                            t = probs[:, n_slot(u), :]
                            nc.gpsimd.tensor_tensor(t, t, penalty[:, kb, :], ALU.mult).then_inc(a["pen_p"], 1)

            over_batches(pool, body)

        @block.scalar
        def _(act):
            chain = Chain(act, ch["scalar"])
            link = chain.link
            with nc.allow_non_contiguous_dma(reason="small bias and gate loads"):
                loads = [
                    (wraw[:, 0, :, :], io["Wqkv"].rearrange("k (t n) -> k t n", t=3)),
                    (wraw[:, 1, 0, :], io["Wq"]), (wraw[:, 1, 1, :], io["Wk"]), (wraw[:, 1, 2, :], io["Wv"]),
                    (wout[:, :], io["Wout"]),
                    (ew[:, :, :], io["expert_w"].rearrange("e h d -> h e d")),
                    (wgate[:, 0, :], io["gate_w"].rearrange("e d -> d e")),
                    (wgate[:, 1, :], io["router_w"]),
                    (bgate[:, :], io["gate_b"].partition_broadcast(P)),
                    (eb[:, :], io["expert_b"].rearrange("e h -> h e")),
                    (bv[:, 0, :], io["bqkv"][2 * D:3 * D].partition_broadcast(P)),
                    (bv[:, 1, :], io["bv"].partition_broadcast(P)),
                    (bo[:, :], io["bout"].rearrange("(n o) -> n o", o=1)),
                    (wg[:, :], io["Wg"]),
                    (bg[:, :], io["bg"].partition_broadcast(P)),
                ]
                for l, t, v in ((0, 0, io["bqkv"][0:D]), (0, 1, io["bqkv"][D:2 * D]), (1, 0, io["bq"]), (1, 1, io["bk"])):
                    for d in range(HD):
                        loads.append((bqk[d * NH:(d + 1) * NH, l, t:t + 1],
                                      v.rearrange("(h d) -> d h", d=HD)[d].rearrange("(h o) -> h o", o=1)))
                for dst, src in loads:
                    act.dma_start(dst, src).then_inc(d_w, 16)
                assert len(loads) == LOADS

            def norm_scalar(l):
                act.wait_ge(var_ok[l], 1)
                nc.scalar.activation(lnw[:, 4, :], lnw[:, 3, :], ACT.Sqrt).then_inc(std_ok[l], 1)

                def body(t, first):
                    for half in range(2):
                        b = 2 * t + half
                        act.wait_ge(tr_ok[l], b + 1)
                        if not first:
                            act.wait_ge(xnT_ok[l], b - 1)
                            act.wait_ge(logits_ok[l], KB * (b - 1))
                        nc.scalar.activation(xts[half], banks[half][:, :].rearrange("p (t d) -> p t d", t=KB),
                                             ACT.Copy).then_inc(xts_ok[l], 1)

                body(0, True)
                with act.Fori(1, B // 2) as t:
                    body(t, False)

            def attention_scalar(l):
                a = A[l]

                def prepare(b, what):
                    if what == "xb":
                        nc.scalar.activation(xb[:, :], xnT[:, bass.ds(b * S, S)], ACT.Copy).then_inc(a["xb_ok"], 1)
                        return
                    t = 0 if what[0] == "q" else 1
                    if what in ("q", "k"):
                        act.wait_ge(a["qk_ps"], 2 * b + t + 1)
                        nc.scalar.activation(qk_f[:, t, :], m0[:, :], ACT.Identity, bias=bqk[:, l, t:t + 1],
                                             scale=(1.0, HD ** -0.5)[t]).then_inc(a[what + "_used"], 1)
                    elif what in ("q_hi", "k_hi"):
                        act.wait_ge(a[what[0] + "_used"], b + 1)
                        nc.scalar.activation(parts[:, 3 * t, :], qk_f[:, t, :], ACT.Copy).then_inc(a["hi_ok"], 1)
                    elif what in ("q_mid", "k_mid"):
                        act.wait_ge(a["res_ok"], 2 * b + t + 1)
                        nc.scalar.activation(parts[:, 3 * t + 1, :], qk_r[:, t, :], ACT.Copy).then_inc(a["mid_ok"], 1)
                    elif what == "gate":
                        act.wait_ge(a["zc_ps"], b + 1)
                        nc.scalar.activation(zc[:, 0, :], m0[:, 0:KB], ACT.Exp, bias=nbg[:, :], scale=-1.0
                                             ).then_inc(a["ze_ok"], 1)
                    elif what == "reach":
                        act.wait_ge(a["zc_ok"], b + 1)
                        nc.scalar.activation(zc[:, 6, :], zc[:, 1, :], ACT.Exp, scale=-float(np.log(S - 2.0)),
                                             bias=lnbase[:, :]).then_inc(a["reach_ok"], 1)
                    elif what == "gates":
                        act.wait_ge(a["zr_ps"], b + 1)
                        nc.scalar.activation(zrow[:, :], m0[:, :], ACT.Copy).then_inc(a["zr_ok"], 1)
                    else:
                        i = int(what[-1])
                        n = KB * b + i
                        if what[:-1] == "u":
                            if i == 0:
                                act.wait_ge(a["zr_ok"], b + 1)
                            if not (isinstance(b, int) and n == 0):
                                act.wait_ge(a["penq_ok"], n)
                            nc.scalar.activation(pw[:, 0, :], zrow[:, :], ACT.Relu, scale=zc[:, 2, i:i + 1],
                                                 bias=zc[:, 3, i:i + 1])
                        elif what[:-1] == "t":
                            nc.scalar.activation(pw[:, 1, :], zrow[:, :], ACT.Relu, scale=zc[:, 5, i:i + 1],
                                                 bias=zc[:, 4, i:i + 1])
                        elif what[:-1] == "s":
                            if i == 0:
                                act.wait_ge(a["reach_ok"], b + 1)
                            lo = (KB - 1 - i) * P
                            nc.scalar.activation(pw[:, 2, :], dist[:, lo:lo + S], ACT.Identity,
                                                 bias=zc[:, 6, i:i + 1]).then_inc(a["penx_ok"], 1)
                        elif what[:-1] == "raw":
                            act.wait_ge(a["pent_ps"], n + 1)
                            if i == 0 and not (isinstance(b, int) and b == 0):
                                act.wait_ge(a["pen_ok"], KB * b)
                            nc.scalar.activation(penalty_raw[:, :, i * P:(i + 1) * P],
                                                 m0[:, :].rearrange("p (k q) -> p k q", k=KB), ACT.Copy
                                                 ).then_inc(a["penraw_ok"], 1)

                def put_v(g):
                    nc.scalar.activation(vexp[:, g, :, :, 0:HD], vtok[:, :, HG * g:HG * g + HG, :], ACT.Copy
                                         ).then_inc(a["vexp_ok"], 1)

                def shift_hi(G, g):
                    act.wait_ge(a["mt_ps"], G + 1)
                    nc.scalar.activation(mrow[:, g, 0, :], m0[0:UN, 0:P], ACT.Copy, scale=-1.0).then_inc(a["mhi_ok"], 1)

                for what in ("xb", "q", "q_hi", "k", "k_hi", "q_mid", "k_mid"):
                    prepare(0, what)
                act.wait_ge(a["v_ok"], 1)
                act.wait_ge(cleared, 4)
                for g in range(NG):
                    put_v(g)
                if l == 1:
                    for what in ("gate", "reach", "gates"):
                        prepare(0, what)
                    for i in range(KB):
                        for what in "uts":
                            prepare(0, f"{what}{i}")
                        prepare(0, f"raw{i}")
                shift_hi(0, 0)
                lag = LAG[l]

                def tail(G, g):
                    act.wait_ge(a["av_ps"], UN * G)
                    if not isinstance(G, int) or G >= 2:
                        act.wait_ge(a["avt_ps"], G - 1)
                    nc.scalar.activation(av_s[:, :], avb[g % 2][:, :], ACT.Copy).then_inc(a["av_s_ok"], 1)

                def body(b, first, last):
                    for g in range(NG):
                        G = 4 * b + g
                        for u in range(UN):
                            n = UN * G + u
                            act.wait_ge(a["sc_ps"], n + 1)
                            if not first or UN * g + u >= PRING:
                                act.wait_ge(a["av_ps"], n - PRING + 1)
                            lo = unit_key(u)[0] * P if l == 0 else 0
                            nc.scalar.activation(probs[:, n_slot(u), lo:S], scb[u % 2][:, 0:S - lo], ACT.Exp
                                                 ).then_inc(a["exp_ok"], 1)
                            if u == 4 and not (last and g == NG - 1):
                                shift_hi(G + 1, (g + 1) % NG)
                            if u == lag + 1 and not (first and g == 0):
                                tail(G, (g - 1) % NG)
                            if u == lag + 2 and not (first if g == 0 else last):
                                act.wait_ge(a["v_ok"], (b if g == 0 else b + 1) + 1)
                                put_v((g - 1) % NG)
                            if last:
                                continue
                            what = SCALAR_NEXT[l].get((g, u))
                            if what == "xb":
                                act.wait_ge(a["v_ps"], b + 1)
                                if l == 1:
                                    act.wait_ge(a["zc_ps"], b + 1)
                            if what == "q_hi":
                                act.wait_ge(a["spilled"], 16 * (b + 1))
                            if what:
                                prepare(b + 1, what)

                over_batches(act, body)
                tail(B * NG, (NG - 1) % NG)

            norm_scalar(0)
            for e in range(E):
                act.wait_ge(ewT_ps, e // 4 + 1)
                if e == 0:
                    act.wait_ge(cnt_ok, 1)
                nc.scalar.activation(ewT[:, e, :], banks[3 + e // 4][:, (e % 4) * P:(e % 4) * P + P], ACT.Copy,
                                     scale=cnt[:, e:e + 1]).then_inc(ewT_ok, 1)
            attention_scalar(0)

            def out_scalar(b, half):
                act.wait_ge(ct_ps, b + 1)
                nc.scalar.activation(av_s[:, :], m0[:, :], ACT.Copy).then_inc(ctT_ok, 1)
                act.wait_ge(op_ps, b + 1)
                nc.scalar.activation(qk_f[:, half, :], banks[6][:, :], ACT.Identity, bias=bsum[:, :]).then_inc(acc0_ok, 1)

            with act.Fori(0, B // 2) as t:
                for half in range(2):
                    out_scalar(2 * t + half, half)

            def weights_hi(e):
                act.wait_ge(w_in[e % 2], 32 * (e // 2 + 1))
                if e >= 2:
                    act.wait_ge(dn_ps, B * (e - 1))
                for i in range(2):
                    nc.scalar.activation(w_split[:, e % 2, 2 * i, :], w_raw[:, e % 2, i, :], ACT.Copy, scale=W_SCALE
                                         ).then_inc(w_hi_ok, 1)

            norm_scalar(1)
            weights_hi(0)
            act.wait_ge(g_sub, 1)
            nc.scalar.activation(gt[:, 1, :, :], gt[:, 1, :, :], ACT.Exp).then_inc(g_exp, 1)
            attention_scalar(1)

            def experts_pair(e, t, first):
                for half in range(2):
                    n = B * e + 2 * t + half
                    for c in range(FC):
                        act.wait_ge(up_ps, FC * n + c + 1)
                        if c == 0 and not first:
                            act.wait_ge(dn_ps, n - 1)
                        nc.scalar.activation(hidden[half][:, c, :], banks[c][:, :], ACT.Gelu, scale=1.0 / W_SCALE
                                             ).then_inc(hid_ok, 1)
                        act.wait_ge(hid_ok, FC * n + c + 1)
                        nc.scalar.activation(h_split[half][:, 0, c, :], hidden[half][:, c, :], ACT.Copy,
                                             scale=H_SCALE).then_inc(h_hi_ok, 1)

            for e in range(E + 1):
                experts_pair(e, 0, e == 0)
                if e < E:
                    weights_hi(e + 1)
                with act.Fori(1, B // 2) as t:
                    experts_pair(e, t, False)

        @block.vector
        def _(dve):
            chain = Chain(dve, ch["vector"])
            link = chain.link
            vec = nc.vector

            def normalise(l):
                chain.start(chain.base + chain.k)
                with dve.Fori(0, NT) as t:
                    vec.bn_stats(stats[:, t, :], x[:, t, :]).then_inc(ch["vector"], 1)
                chain.k += NT
                dve.wait_ge(ch["vector"], chain.base + chain.k)
                me, qe, mo, qo = (stats[:, :, i] for i in (1, 2, 4, 5))
                mean, dif, var, std = lnw[:, 0, :], lnw[:, 1, :], lnw[:, 3, :], lnw[:, 4, :]
                link(vec.tensor_tensor(mean, me, mo, ALU.add))
                link(vec.tensor_scalar(mean, mean, 0.5, None, ALU.mult))
                link(vec.tensor_tensor(dif, me, mo, ALU.subtract))
                link(vec.tensor_tensor(dif, dif, dif, ALU.mult))
                link(vec.tensor_tensor(var, qe, qo, ALU.add))
                link(vec.tensor_scalar(var, var, 1.0 / D, EPS, ALU.mult, ALU.add))
                vec.scalar_tensor_tensor(var, dif, 0.25, var, ALU.mult, ALU.add).then_inc(var_ok[l], 1)
                dve.wait_ge(std_ok[l], 1)
                link(vec.reciprocal(lnw[:, 2, :], std))

                with dve.Fori(0, B) as b:
                    for i in range(KB):
                        t = KB * b + i
                        last = vec.tensor_scalar(xn[:, bass.ds(t, 1), :].rearrange("p t d -> p (t d)"),
                                                 x[:, bass.ds(t, 1), :].rearrange("p t d -> p (t d)"),
                                                 lnw[:, 0, bass.ds(t, 1)],
                                                 lnw[:, 2, bass.ds(t, 1)], ALU.subtract, ALU.mult)
                    last.then_inc(xn_ok[l], 1)
                dve.wait_ge(xn_ok[l], B)

                with dve.Fori(0, B // 2) as t:
                    for half in range(2):
                        b = 2 * t + half
                        if l == 1:
                            dst = x[:, bass.ds(KB * b, KB), :]
                            vec.tensor_tensor(dst, dst, xn[:, bass.ds(KB * b, KB), :], ALU.add)
                        dve.wait_ge(xts_ok[l], b + 1)
                        vec.tensor_copy(xnT[:, bass.ds(b * S, S)], xts[half].rearrange("p t d -> p (t d)")
                                        ).then_inc(xnT_ok[l], 1)

            def top2(work):
                g, tmp, hot, hot2 = gt[:, work, :, :], gt[:, 3, :, :], gt[:, 2, :, :], gt[:, 3, :, :]
                best, at = gs[:, 2, :], gs[:, 3, :]
                wide = lambda v: v.unsqueeze(2).broadcast_to((P, NT, E))
                idx = eidx[:, :].unsqueeze(1).broadcast_to((P, NT, E))

                def onehot(src, dst):
                    link(vec.reduce_max(best, src, AX.X))
                    link(vec.tensor_tensor(tmp, src, wide(best), ALU.is_equal))
                    link(vec.tensor_tensor(tmp, tmp, idx, ALU.mult))
                    link(vec.tensor_reduce(at, tmp, AX.X, ALU.min))
                    link(vec.tensor_tensor(dst, idx, wide(at), ALU.is_equal))

                onehot(g, hot)
                rest = gt[:, 1 - work, :, :]
                link(vec.scalar_tensor_tensor(rest, hot, -3.0e38, g, ALU.mult, ALU.add))
                onehot(rest, hot2)
                return g, hot, hot2

            def attention_vector(l, base):
                a = A[l]
                lag = LAG[l]

                def prepare(b, what):
                    t = 0 if what[0] == "q" else 1
                    if what in ("q_res", "k_res"):
                        dve.wait_ge(a["hi_ok"], 2 * b + t + 1)
                        vec.tensor_tensor(qk_r[:, t, :], qk_f[:, t, :], parts[:, 3 * t, :], ALU.subtract
                                          ).then_inc(a["res_ok"], 1)
                    elif what in ("q_lo", "k_lo"):
                        dve.wait_ge(a["mid_ok"], 2 * b + t + 1)
                        vec.tensor_tensor(parts[:, 3 * t + 2, :], qk_r[:, t, :], parts[:, 3 * t + 1, :], ALU.subtract
                                          ).then_inc(a["lo_ok"], 1)
                    elif what == "v":
                        dve.wait_ge(a["v_ps"], b + 1)
                        bias = bv[:, l, :].unsqueeze(1).broadcast_to((P, KB, D))
                        vec.tensor_tensor(vtok[:, :, :, :].rearrange("p k h d -> p k (h d)"),
                                          m0[:, :].rearrange("p (k n) -> p k n", k=KB), bias, ALU.add
                                          ).then_inc(a["v_ok"], 1)
                    elif what == "gate":
                        dve.wait_ge(a["ze_ok"], b + 1)
                        link(vec.tensor_scalar(zc[:, 0, :], zc[:, 0, :], 1.0, None, ALU.add))
                        link(vec.reciprocal(zc[:, 1, :], zc[:, 0, :]))
                        link(vec.tensor_scalar(zc[:, 2, :], zc[:, 1, :], -1.0, None, ALU.add))
                        vec.tensor_tensor(zc[:, 3, :], zc[:, 2, :], zc[:, 2, :], ALU.mult)
                        vec.tensor_tensor(zc[:, 4, :], zc[:, 1, :], zc[:, 1, :], ALU.mult)
                        vec.tensor_scalar(zc[:, 5, :], zc[:, 1, :], -1.0, None, ALU.mult).then_inc(a["zc_ok"], 1)
                    elif what[:-1] == "sum":
                        i = int(what[-1])
                        dve.wait_ge(a["penx_ok"], KB * b + i + 1)
                        link(vec.scalar_tensor_tensor(pw[:, 0, :], pw[:, 0, :], zc[:, 1, i:i + 1], pw[:, 1, :],
                                                      ALU.add, ALU.subtract))
                    elif what[:-1] == "product":
                        i = int(what[-1])
                        n = KB * b + i
                        if not (isinstance(b, int) and n == 0):
                            dve.wait_ge(a["pent_ps"], n)
                        vec.scalar_tensor_tensor(pw[:, 3, :], pw[:, 2, :], 1.0, pw[:, 0, :], ALU.min, ALU.mult
                                                 ).then_inc(a["penq_ok"], 1)
                    elif what[:-1] == "put":
                        kb = int(what[-1])
                        if kb == 0:
                            dve.wait_ge(a["penraw_ok"], KB * b + KB)
                        if not (isinstance(b, int) and b == 0):
                            dve.wait_ge(a["pen_p"], N_POOL * (NG * b - 1)
                                        + sum(w not in ON_DVE for w in range(HG * (kb + 1))))
                        vec.tensor_scalar(penalty[:, kb, :], penalty_raw[:, kb, :], 1e-32, None, ALU.max
                                          ).then_inc(a["pen_ok"], 1)

                def maxima(n, G, g, u):
                    j, qb = unit_query(u)
                    width = (qb + 1) * P if l == 0 else S
                    dve.wait_ge(a["mx_ps"], n + 1)
                    vec.reduce_max(mx[:, g, u:u + 1], max_bank(g, u)[:, 0:width], AX.X).then_inc(a["mx_ok"], 1)

                def shift_mid(G, g):
                    dve.wait_ge(a["mhi_ok"], G + 1)
                    vec.scalar_tensor_tensor(mrow[:, g, 1, :], m0[0:UN, 0:P], -1.0, mrow[:, g, 0, :],
                                             ALU.mult, ALU.subtract).then_inc(a["mrow_ok"], 1)

                def tail(G, g):
                    dve.wait_ge(a["avt_ps"], G)
                    ps = m0[:, :].rearrange("p (q j c) -> p q j c", q=KB, j=HG)
                    link(vec.reciprocal(rec[:, :, :], ps[:, :, :, HD]))
                    ratio = rec[:, :, :].unsqueeze(3).broadcast_to((P, KB, HG, HD))
                    bt = (G - 1) // NG if isinstance(G, int) else None
                    return ps, ratio

                def tail_to(G, g, bt):
                    ps, ratio = tail(G, g)
                    cols = slice(g * HG * HD, (g + 1) * HG * HD)
                    if l == 0:
                        dst = context[:, bass.ds(bt * KB, KB), cols].rearrange("p q (j d) -> p q j d", j=HG)
                        vec.tensor_tensor(dst, ps[:, :, :, 0:HD], ratio, ALU.mult).then_inc(a["norm_ok"], 1)
                    else:
                        link(vec.tensor_tensor(ctx_t[:, :, :, :], ps[:, :, :, 0:HD], ratio, ALU.mult))
                        dst = x[:, bass.ds(bt * KB, KB), cols]
                        vec.tensor_tensor(dst, dst, ctx_t[:, :, :, :].rearrange("p q j d -> p q (j d)"), ALU.add
                                          ).then_inc(a["norm_ok"], 1)

                for what in ("q_res", "k_res", "q_lo", "k_lo", "v"):
                    prepare(0, what)
                if l == 1:
                    prepare(0, "gate")
                for G in range(2):
                    for u in range(UN):
                        maxima(UN * G + u, G, G, u)
                        if l == 1 and u % 8 == 7:
                            i = (UN * G + u) // 8
                            prepare(0, f"sum{i}")
                            prepare(0, f"product{i}")
                if l == 1:
                    for kb in range(KB):
                        prepare(0, f"put{kb}")
                shift_mid(0, 0)
                start = chain.base + chain.k
                per = NG if l == 0 else 2 * NG + 3 + KB

                def body(b, first, last):
                    chain.start(start + per * b)
                    for g in range(NG):
                        G = 4 * b + g
                        for u in range(UN):
                            if not (last and g >= 2):
                                if u == 0 and not (first and g < 2):
                                    dve.wait_ge(a["mt_ps"], G - 1)
                                maxima(UN * (G + 2) + u, G + 2, (g + 2) % NG, u)
                            if l == 1:
                                v = u - 1
                                if v in ON_DVE:
                                    dve.wait_ge(a["exp_ok"], UN * G + v + 1)
                                    t = probs[:, n_slot(v), :]
                                    vec.tensor_tensor(t, t, penalty[:, unit_key(v)[0], :], ALU.mult
                                                      ).then_inc(a["pen_v"], 1)
                            if l == 1 and g == 0 and 0 < u < KB and not first:
                                prepare(b, f"put{u}")
                            if u == 5 and not (last and g == NG - 1):
                                shift_mid(G + 1, (g + 1) % NG)
                            if u == lag + 5 and not (first and g == 0):
                                tail_to(G, (g - 1) % NG, b if g else b - 1)
                            if last:
                                continue
                            what = VECTOR_NEXT[l].get((g, u))
                            if what == "v":
                                dve.wait_ge(a["vexp_ok"], NG * b + NG)
                            if what:
                                prepare(b + 1, what)
                    chain.fill(per)

                over_batches(dve, body)
                chain.start(start + per * B)
                tail_to(B * NG, NG - 1, B - 1)

            dve.wait_ge(consts, 8)
            vec.tensor_copy(eidx[:, :], eidx_i[:, :]).then_inc(consts, 1)
            link(vec.tensor_copy(dist[:, :], disti[:, :]))
            link(vec.scalar_tensor_tensor(dist[:, :], dist[:, :], -1.0, dist[:, :], ALU.mult, ALU.max))
            vec.tensor_scalar(dist[:, :], dist[:, :], -1.0, 2.0, ALU.mult, ALU.add).then_inc(consts, 1)
            dve.wait_ge(d_x, 64)
            normalise(0)
            dve.wait_ge(d_w, 16 * LOADS)
            for l in (0, 1):
                for t in range(2):
                    vec.tensor_copy(wproj[:, l, t, :].rearrange("p (d h) -> p d h", d=HD),
                                    wraw[:, l, t, :].rearrange("p (h d) -> p d h", d=HD)).then_inc(wready, 1)
                vec.tensor_copy(wproj[:, l, 2, :], wraw[:, l, 2, :]).then_inc(wready, 1)
                vec.tensor_scalar(bqk[:, l, 1:2], bqk[:, l, 1:2], HD ** -0.5, None, ALU.mult).then_inc(wready, 1)
            vec.tensor_scalar(nbg[:, :], bg[:, :], -1.0, None, ALU.mult).then_inc(wready, 1)

            dve.wait_ge(logits_ok[0], NT)
            gb = bgate[:, :].unsqueeze(1).broadcast_to((P, NT, E))
            dve.wait_ge(consts, 10)
            link(vec.tensor_tensor(gt[:, 0, :, :], banks[2][:, 0:NT * E].rearrange("p (t e) -> p t e", e=E), gb, ALU.add))
            g, hot, hot2 = top2(0)
            vec.tensor_tensor(gt[:, 0, :, :], hot, hot2, ALU.add).then_inc(mask_ok, 1)
            dve.wait_ge(cnt_ps, 1)
            link(vec.reduce_sum(cnt[:, :], banks[2][:, 0:NT * E].rearrange("p (t e) -> p e t", e=E), AX.X))
            link(vec.tensor_scalar(cnt[:, :], cnt[:, :], 1.0 / (2 * TOKENS), None, ALU.mult))
            link(vec.scalar_tensor_tensor(nb[:, :], cnt[:, :], -1.0, eb[:, :], ALU.mult, ALU.mult))
            link(vec.reduce_sum(bsum[:, :], nb[:, :], AX.X))
            vec.tensor_tensor(bsum[:, :], bo[:, :], bsum[:, :], ALU.subtract).then_inc(cnt_ok, 1)

            attention_vector(0, 0)

            dve.wait_ge(A[0]["norm_ok"], B * NG)

            def contexts_out(b, half):
                if not (isinstance(b, int) and b < 2):
                    dve.wait_ge(ct_ps, b - 1)
                vec.tensor_copy(xts[half], context[:, bass.ds(b * KB, KB), :]).then_inc(ctile_ok, 1)

            def stream_add(b):
                dve.wait_ge(yT_ps, b + 1)
                dst = x[:, bass.ds(b * KB, KB), :]
                vec.tensor_tensor(dst, dst, banks[4][:, :].rearrange("p (t d) -> p t d", t=KB), ALU.add
                                  ).then_inc(x1_ok, 1)

            def out_pair(t, first, last):
                for half in range(2):
                    b = 2 * t + half
                    if not (last and half == 1):
                        contexts_out(b + 1, 1 - half)
                    dve.wait_ge(acc0_ok, b + 1)
                    acc = qk_f[:, half, :]
                    for e in range(E):
                        dve.wait_ge(ff_ps, E * b + e + 1)
                        vec.scalar_tensor_tensor(acc, banks[e % 4][:, :], nb[:, e:e + 1], acc, ALU.max, ALU.add
                                                 ).then_inc(acc_ok, 1)
                        if e == 3 and not (first and half == 0):
                            stream_add(b - 1)
                        dve.wait_ge(acc_ok, E * b + e + 1)

            contexts_out(0, 0)
            out_pair(0, True, False)
            with dve.Fori(1, B // 2 - 1) as t:
                out_pair(t, False, False)
            out_pair(B // 2 - 1, False, True)
            stream_add(B - 1)
            dve.wait_ge(x1_ok, B)

            def weights_lo(e):
                for i in range(2):
                    dve.wait_ge(w_hi_ok, 2 * e + i + 1)
                    vec.scalar_tensor_tensor(w_split[:, e % 2, 2 * i + 1, :], w_raw[:, e % 2, i, :], W_SCALE,
                                             w_split[:, e % 2, 2 * i, :], ALU.mult, ALU.subtract).then_inc(w_lo_ok, 1)

            normalise(1)
            dve.wait_ge(logits_ok[1], NT)
            wide = lambda v: v.unsqueeze(2).broadcast_to((P, NT, E))
            lg = banks[2][:, 0:NT * E].rearrange("p (t e) -> p t e", e=E)
            link(vec.reduce_max(gs[:, 0, :], lg, AX.X))
            vec.tensor_tensor(gt[:, 1, :, :], lg, wide(gs[:, 0, :]), ALU.subtract).then_inc(g_sub, 1)
            dve.wait_ge(g_exp, 1)
            link(vec.reduce_sum(gs[:, 0, :], gt[:, 1, :, :], AX.X))
            link(vec.reciprocal(gs[:, 1, :], gs[:, 0, :]))
            link(vec.tensor_tensor(gt[:, 1, :, :], gt[:, 1, :, :], wide(gs[:, 1, :]), ALU.mult))
            g, hot, hot2 = top2(1)
            link(vec.tensor_tensor(hot, hot, hot2, ALU.add))
            link(vec.scalar_tensor_tensor(gt[:, 2, :, :], hot, 1.0 / (W_SCALE * H_SCALE), g, ALU.mult, ALU.mult))
            weights_lo(0)

            attention_vector(1, 0)
            dve.wait_ge(A[1]["norm_ok"], B * NG)

            dve.sem_inc(add_ok, 2)

            def halves_lo(n, half):
                for c in range(FC):
                    dve.wait_ge(h_hi_ok, FC * n + c + 1)
                    vec.scalar_tensor_tensor(h_split[half][:, 1, c, :], hidden[half][:, c, :], H_SCALE,
                                             h_split[half][:, 0, c, :], ALU.mult, ALU.subtract).then_inc(h_lo_ok, 1)

            def expert_add(e, n, b, half):
                dve.wait_ge(dn_ps, n + 1)
                for i in range(KB):
                    t = KB * b + i
                    src = banks[4 + half][:, i * P:(i + 1) * P]
                    gate = 1.0 / (W_SCALE * H_SCALE) if e == 0 else gt[:, 2, t, e - 1:e]
                    ins = vec.scalar_tensor_tensor(x[:, t, :], src, gate, x[:, t, :], ALU.mult, ALU.add)
                ins.then_inc(add_ok, 1)

            for e in range(E + 1):
                n = B * e
                halves_lo(n, 0)
                halves_lo(n + 1, 1)
                if e < E:
                    weights_lo(e + 1)
                expert_add(e, n, 0, 0)
                with dve.Fori(1, B // 2) as t:
                    for half in range(2):
                        halves_lo(n + 2 * t + half, half)
                        expert_add(e, n + 2 * t + half - 1, 2 * t + half - 1, 1 - half)
                expert_add(e, n + B - 1, B - 1, 1)
                dve.wait_ge(add_ok, 2 + n + B)

        @block.tensor
        def _(pe):
            mm = nc.tensor.matmul
            transpose = nc.tensor.transpose

            def normalise(l):
                if l == 0:
                    pe.wait_ge(consts, 10)
                    pe.wait_ge(d_w, 16 * LOADS)
                for t in range(B // 2):
                    for half in range(2):
                        b = 2 * t + half
                        pe.wait_ge(xn_ok[l], b + 1)
                        if b >= 2:
                            pe.wait_ge(xts_ok[l], b - 1)
                        for i in range(KB):
                            last = transpose(banks[half][:, i * P:(i + 1) * P], xn[:, KB * b + i, :], ident[:, :])
                        last.then_inc(tr_ok[l], 1)
                    for half in range(2):
                        b = 2 * t + half
                        pe.wait_ge(xts_ok[l], b + 1)
                        for i in range(KB):
                            t8 = (KB * b + i) * E
                            mm(banks[2][:, t8:t8 + E], xts[half][:, i, :], wgate[:, l, :],
                               start=True, stop=True).then_inc(logits_ok[l], 1)

            def attention_tensor(l):
                a = A[l]
                lag = LAG[l]

                spare_last = [None]

                def spare(what, b):
                    if spare_last[0] is not None:
                        pe.wait_ge(*spare_last[0])
                    if what == "q":
                        pe.wait_ge(a["xb_ok"], b + 1)
                    if what in ("q", "k"):
                        t = 0 if what == "q" else 1
                        mm(m0[:, :], wproj[:, l, t, :], xb[:, :], start=True, stop=True).then_inc(a["qk_ps"], 1)
                        spare_last[0] = (a[what + "_used"], b + 1)
                    elif what == "v":
                        for kb in range(KB):
                            last = mm(m0[:, kb * P:(kb + 1) * P], xb[:, kb * P:(kb + 1) * P], wproj[:, l, 2, :],
                                      start=True, stop=True)
                        last.then_inc(a["v_ps"], 1)
                        spare_last[0] = (a["v_ok"], b + 1)
                    elif what == "gate":
                        for kb in range(KB):
                            last = mm(m0[:, kb:kb + 1], xb[:, kb * P:(kb + 1) * P], wg[:, :], start=True, stop=True)
                        last.then_inc(a["zc_ps"], 1)
                        spare_last[0] = (a["ze_ok"], b + 1)
                    elif what == "gates":
                        pe.wait_ge(a["zc_ok"], b + 1)
                        for kb in range(KB):
                            last = mm(m0[:, kb * P:(kb + 1) * P], zc[:, 1, kb:kb + 1].broadcast_to((P, P)),
                                      ident[:, :], start=True, stop=True)
                        last.then_inc(a["zr_ps"], 1)
                        spare_last[0] = (a["zr_ok"], b + 1)
                    elif what.startswith("penalty"):
                        i = int(what[-1])
                        pe.wait_ge(a["penq_ok"], KB * b + i + 1)
                        for kb in range(KB):
                            last = transpose(m0[:, kb * P:(kb + 1) * P], pw[:, 3, kb * P:(kb + 1) * P], ident[:, :])
                        last.then_inc(a["pent_ps"], 1)
                        spare_last[0] = (a["penraw_ok"], KB * b + i + 1)

                def turn_maxima(G, g):
                    if spare_last[0] is not None:
                        pe.wait_ge(*spare_last[0])
                    pe.wait_ge(a["mx_ok"], UN * (G + 1))
                    transpose(m0[0:UN, 0:P], mx[:, g, :], ident[:, :]).then_inc(a["mt_ps"], 1)
                    spare_last[0] = (a["mrow_ok"], G + 1)

                def turn_context(G):
                    if spare_last[0] is not None:
                        pe.wait_ge(*spare_last[0])
                    pe.wait_ge(a["av_s_ok"], G)
                    for qb in range(KB):
                        last = transpose(m0[:, qb * P:(qb + 1) * P], av_s[:, qb * P:(qb + 1) * P], ident[:, :])
                    last.then_inc(a["avt_ps"], 1)
                    spare_last[0] = (a["norm_ok"], G)

                def score_max(n, g, u, free):
                    j, qb = unit_query(u)
                    bank = max_bank(g, u)
                    if free is not None:
                        pe.wait_ge(a["mx_ok"], free)
                    lhs = qst[0:SHIFT_ROW, g, j * S + qb * P:j * S + (qb + 1) * P]
                    if l == 0:
                        mm(bank[:, 0:(qb + 1) * P], lhs, kst[0:SHIFT_ROW, g, j * S:j * S + (qb + 1) * P],
                           start=True, stop=False)
                        mm(bank[:, qb * P:(qb + 1) * P], ident16[:, :], mask_q[:, :], start=False, stop=True
                           ).then_inc(a["mx_ps"], 1)
                    else:
                        mm(bank[:, :], lhs, kst[0:SHIFT_ROW, g, j * S:(j + 1) * S], start=True, stop=True
                           ).then_inc(a["mx_ps"], 1)

                def score(n, g, u, free):
                    kb, j = unit_key(u)
                    bank = scb[u % 2]
                    if free is not None:
                        pe.wait_ge(a["exp_ok"], free)
                    rows = slice(0, SHIFT_ROW + 2)
                    lhs = kst[rows, g, j * S + kb * P:j * S + (kb + 1) * P]
                    if l == 0:
                        mm(bank[:, 0:S - kb * P], lhs, qst[rows, g, j * S + kb * P:(j + 1) * S], start=True, stop=False)
                        mm(bank[:, 0:P], ident16[:, :], mask_k[:, :], start=False, stop=True).then_inc(a["sc_ps"], 1)
                    else:
                        mm(bank[:, :], lhs, qst[rows, g, j * S:(j + 1) * S], start=True, stop=True).then_inc(a["sc_ps"], 1)

                def weigh(n, G, g, u):
                    kb, j = unit_key(u)
                    if l == 0:
                        pe.wait_ge(a["exp_ok"], n + 1)
                    elif u in ON_DVE:
                        pe.wait_ge(a["pen_v"], len(ON_DVE) * G + sum(v <= u for v in ON_DVE))
                    else:
                        pe.wait_ge(a["pen_p"], (UN - len(ON_DVE)) * G + sum(v <= u for v in range(UN) if v not in ON_DVE))
                    lo = kb * P if l == 0 else 0
                    last = mm(avb[g % 2][32 * j:32 * j + 32, lo:S], vexp[:, g, kb, j, :], probs[:, n_slot(u), lo:S],
                              start=(kb == 0), stop=(kb == KB - 1))
                    last.then_inc(a["av_ps"], 1)

                pe.wait_ge(wready, 9)
                pe.wait_ge(xnT_ok[l], B)
                for what in ("q", "k", "v"):
                    spare(what, 0)
                if l == 1:
                    spare("gate", 0)
                    spare("gates", 0)
                for G in range(2):
                    pe.wait_ge(a[f"stacked{G}"], 6 * 16)
                    for u in range(UN):
                        n = UN * G + u
                        score_max(n, G, u, n - max_bank_last(G, u) + 1 if n >= 3 else None)
                        if l == 1 and n % 8 == 3 and n > 8:
                            spare(f"penalty{n // 8 - 1}", 0)
                if l == 1:
                    spare(f"penalty{KB - 1}", 0)
                turn_maxima(0, 0)

                def body(b, first, last):
                    if not first:
                        spare_last[0] = (a["norm_ok"], NG * b - 1) if l == 0 else (a["penraw_ok"], KB * (b + 1))
                    for g in range(NG):
                        G = 4 * b + g
                        for u in range(UN):
                            if not (last and g >= 2):
                                g2, n2 = (g + 2) % NG, UN * (G + 2) + u
                                if u == 0:
                                    pe.wait_ge(a[f"stacked{g2}"], 6 * 16 * ((b if g < 2 else b + 1) + 1))
                                score_max(n2, g2, u, n2 - max_bank_last(g2, u) + 1)
                            if u == 0:
                                pe.wait_ge(a[f"shift{g}"], 32 * (b + 1))
                            n = UN * G + u
                            score(n, g, u, None if first and g == 0 and u < 2 else n - 1)
                            if u >= lag:
                                if u == lag and not (first and g < 1):
                                    if not (first and g < 2):
                                        pe.wait_ge(a["av_s_ok"], G - 1)
                                if u == lag:
                                    pe.wait_ge(a["vexp_ok"], vexp_needed(b, g, first))
                                weigh(n - lag, G, g, u - lag)
                            elif not (first and g == 0):
                                weigh(n - lag, G - 1, (g - 1) % NG, UN + u - lag)
                            every = SPARE[l]["every"].get(u)
                            if every == "maxima" and not (last and g == NG - 1):
                                turn_maxima(G + 1, (g + 1) % NG)
                            if every == "contexts" and not (first and g == 0):
                                turn_context(G)
                            if (g, u) in SPARE[l]["next"] and not last:
                                spare(SPARE[l]["next"][g, u], b + 1)

                def vexp_needed(b, g, first):
                    return NG if first else NG * b + g + 1

                over_batches(pe, body)
                for u in range(UN - lag, UN):
                    weigh(UN * (NG * B - 1) + u, NG * B - 1, NG - 1, u)
                turn_context(NG * B)

            normalise(0)
            for e in range(E):
                last = transpose(banks[3 + e // 4][:, (e % 4) * P:(e % 4) * P + P], ew[:, e, :], ident[:, :])
                if e % 4 == 3:
                    last.then_inc(ewT_ps, 1)
            pe.wait_ge(mask_ok, 1)
            mm(banks[2][:, 0:NT * E], ones[:, :], gt[:, 0, :, :].rearrange("p t e -> p (t e)"),
               start=True, stop=True).then_inc(cnt_ps, 1)
            pe.wait_ge(cnt_ok, 1)
            pe.wait_ge(ewT_ok, E)
            attention_tensor(0)

            def turn_out(b, half):
                pe.wait_ge(ctile_ok, b + 1)
                if not (isinstance(b, int) and b == 0):
                    pe.wait_ge(ctT_ok, b)
                for i in range(KB):
                    last = transpose(m0[:, i * P:(i + 1) * P], xts[half][:, i, :], ident[:, :])
                last.then_inc(ct_ps, 1)

            def project(b):
                pe.wait_ge(ctT_ok, b + 1)
                if not (isinstance(b, int) and b == 0):
                    pe.wait_ge(acc0_ok, b)
                mm(banks[6][:, :], wout[:, :], av_s[:, :], start=True, stop=True).then_inc(op_ps, 1)

            def turn_back(b, half):
                pe.wait_ge(acc_ok, E * b + E)
                if not (isinstance(b, int) and b == 0):
                    pe.wait_ge(x1_ok, b)
                for i in range(KB):
                    last = transpose(banks[4][:, i * P:(i + 1) * P], qk_f[:, half, i * P:(i + 1) * P], ident[:, :])
                last.then_inc(yT_ps, 1)

            def out_pair(t, first, last):
                for half in range(2):
                    b = 2 * t + half
                    for e in range(E):
                        if not (first and half == 0 and e < 4):
                            pe.wait_ge(acc_ok, E * b + e - 3)
                        mm(banks[e % 4][:, :], ewT[:, e, :], xnT[:, bass.ds(b * S, S)], start=True, stop=True
                           ).then_inc(ff_ps, 1)
                        if e == 3:
                            if not (first and half == 0):
                                turn_back(b - 1, 1 - half)
                            if not (last and half == 1):
                                turn_out(b + 1, 1 - half)
                    if not (last and half == 1):
                        project(b + 1)

            pe.wait_ge(A[0]["norm_ok"], B * NG)
            turn_out(0, 0)
            project(0)
            out_pair(0, True, False)
            with pe.Fori(1, B // 2 - 1) as t:
                out_pair(t, False, False)
            out_pair(B // 2 - 1, False, True)
            turn_back(B - 1, 1)
            normalise(1)
            attention_tensor(1)

            HALVES = ((0, 0), (0, 1), (1, 0))

            def up(e, n, tb, first):
                for c in range(FC):
                    if not first:
                        pe.wait_ge(hid_ok, FC * (n - 1) + c + 1)
                    for k, (hw, hx) in enumerate(HALVES):
                        last = mm(banks[c][:, :], w_split[:, e % 2, hw, c * P:(c + 1) * P],
                                  xsplit[:, hx, bass.ds(tb * S, S)], start=(k == 0), stop=(k == 2))
                    last.then_inc(up_ps, 1)

            def down(e, n, half):
                pe.wait_ge(h_lo_ok, FC * n + FC)
                pe.wait_ge(add_ok, n + 1)
                for i in range(KB):
                    for c in range(FC):
                        for k, (hh, hw) in enumerate(HALVES):
                            last = mm(banks[4 + half][:, i * P:(i + 1) * P], h_split[half][:, hh, c, i * P:(i + 1) * P],
                                      w_split[:, e % 2, 2 + hw, c * P:(c + 1) * P],
                                      start=(c == 0 and k == 0), stop=(c == FC - 1 and k == 2))
                last.then_inc(dn_ps, 1)

            pe.wait_ge(A[1]["norm_ok"], B * NG)
            pe.wait_ge(x_lo_ok, 1)
            for e in range(E + 1):
                pe.wait_ge(w_lo_ok, 2 * e + 2)
                up(e, B * e, 0, e == 0)
                with pe.Fori(0, B // 2 - 1) as t:
                    n = B * e + 2 * t
                    up(e, n + 1, 2 * t + 1, False)
                    down(e, n, 0)
                    up(e, n + 2, 2 * t + 2, False)
                    down(e, n + 1, 1)
                n = B * e + B - 2
                up(e, n + 1, B - 1, False)
                down(e, n, 0)
                down(e, n + 1, 1)

    return nc


_ARGS = {
    "x": "L0_attn_x", "Wqkv": "L0_attn_Wqkv", "bqkv": "L0_attn_bqkv", "Wout": "L0_attn_Wout", "bout": "L0_attn_bout",
    "gate_w": "L0_ffn_gate_w", "gate_b": "L0_ffn_gate_b", "expert_w": "L0_ffn_expert_w", "expert_b": "L0_ffn_expert_b",
    "Wq": "L1_attn_Wq", "bq": "L1_attn_bq", "Wk": "L1_attn_Wk", "bk": "L1_attn_bk", "Wv": "L1_attn_Wv", "bv": "L1_attn_bv",
    "Wg": "L1_attn_Wg", "bg": "L1_attn_bg", "shared_up": "L1_ffn_shared_up", "shared_down": "L1_ffn_shared_down",
    "routed_up": "L1_ffn_routed_up", "routed_down": "L1_ffn_routed_down", "router_w": "L1_ffn_router_w",
}


def kernel(**inputs):
    import concourse.bacc as bacc
    from concourse.bass_utils import run_bass_kernel_spmd

    nc = bacc.Bacc("TRN2", target_bir_lowering=False, num_devices=1)
    arrays, io = {}, {}
    for short, name in _ARGS.items():
        a = np.ascontiguousarray(inputs[name])
        arrays["in_" + short] = a
        io[short] = nc.dram_tensor("in_" + short, a.shape, mybir.dt.from_np(a.dtype), kind="ExternalInput").ap()
    out = nc.dram_tensor("out", (B, S, D), F32, kind="ExternalOutput").ap()
    program(nc, io, out)
    r = run_bass_kernel_spmd(nc, [arrays], core_ids=[0])
    return r.results[0]["out"]
```

```python
from contextlib import ExitStack

import numpy as np

import concourse.bass as bass
from concourse import mybir

ALU = mybir.AluOpType
ACT = mybir.ActivationFunctionType
AX = mybir.AxisListType
F32 = mybir.dt.float32
BF16 = mybir.dt.bfloat16
F16 = mybir.dt.float16

P = 128
B, S, D = 8, 512, 128
NH, HD = 16, 8
NT = B * S // P
KB = S // P
NG, HG = 4, 4
UN = KB * HG
E = 8
F = 512
FC = F // P
EPS = 1e-5
SHIFT_ROW = 96
EARLY = B - KB
PRING = 16
LAG = (3, 6)
TOKENS = B * S
W_SCALE, H_SCALE = 64.0, 16.0
LOADS = 15 + 4
ON_DVE = ((2, 6, 10, 14), (2, 6, 10, 14), (6, 10, 14), (2, 5, 11, 14))
ON_POOL = tuple(tuple(u for u in range(UN) if u not in v) for v in ON_DVE)
SHIFT = ((2, 3), (2, 3))
NORM = (10, 10)

SPARE = (
    {"every": {1: "maxima", 9: "contexts"},
     "next": {(0, 4): "q", (0, 6): "k", (0, 13): "v"}},
    {"every": {1: "maxima", 9: "contexts"},
     "next": {(0, 7): "q", (0, 13): "k", (0, 15): "v", (1, 7): "gate", (1, 13): "gates",
              (2, 7): "penalty0", (2, 13): "penalty1", (3, 7): "penalty2", (3, 13): "penalty3"}},
)
SCALAR_NEXT = (
    {(0, 1): "xb", (0, 4): "q", (0, 5): "q_hi", (0, 6): "k", (0, 7): "k_hi", (0, 9): "q_mid", (0, 10): "k_mid"},
    {(0, 5): "xb", (0, 7): "q", (0, 8): "q_hi", (0, 12): "q_mid", (0, 13): "k", (0, 14): "k_hi", (1, 1): "k_mid",
     (1, 7): "gate", (1, 11): "reach", (1, 13): "gates",
     (1, 14): "u0", (1, 15): "t0", (2, 1): "s0", (2, 7): "raw0", (2, 4): "u1", (2, 5): "t1", (2, 6): "s1", (2, 13): "raw1",
     (2, 11): "u2", (2, 12): "t2", (2, 14): "s2", (3, 7): "raw2", (3, 2): "u3", (3, 3): "t3", (3, 5): "s3",
     (3, 13): "raw3"},
)
VECTOR_NEXT = (
    {(0, 6): "q_res", (0, 8): "k_res", (0, 10): "q_lo", (0, 12): "k_lo", (0, 14): "v"},
    {(0, 10): "q_res", (0, 13): "q_lo", (0, 15): "v", (1, 0): "k_res", (1, 3): "k_lo", (1, 9): "gate",
     (2, 2): "sum0", (2, 3): "product0", (2, 8): "sum1", (2, 9): "product1",
     (2, 14): "sum2", (2, 15): "product2", (3, 7): "sum3", (3, 8): "product3", (3, 15): "put0"},
)
SPARE_LAST = ({(0, 14): "counts", (1, 12): "weights0", (1, 14): "weights1"}, {})
SCALAR_LAST = ({(1, 13): "weights0", (1, 15): "weights1"}, {(2, 3): "exponentials"})
VECTOR_LAST = (
    {(0, 1): "best", (0, 6): "second", (0, 10): "mask", (1, 0): "shares"},
    {(2, 1): "shifted", (2, 5): "softmax", (2, 9): "best", (2, 13): "second", (3, 1): "gates"},
)


class Chain:

    def __init__(self, eng, sem):
        self.eng, self.sem, self.base, self.k = eng, sem, 0, 0

    def link(self, ins):
        self.k += 1
        ins.then_inc(self.sem, 1)
        self.eng.wait_ge(self.sem, self.base + self.k)

    def start(self, base):
        self.base, self.k = base, 0

    def fill(self, per):
        assert self.k <= per, self.k
        if self.k < per:
            self.eng.sem_inc(self.sem, per - self.k)


def program(nc, io, out):
    ctx = ExitStack()
    with ctx:
        def sb(name, shape, dt=F32):
            return ctx.enter_context(nc.sbuf_tensor(name, shape, dt))

        def sem(name):
            return ctx.enter_context(nc.semaphore(name))

        x = sb("x", [P, NT, D])
        xnT = sb("xnT", [P, TOKENS])
        big = sb("big", [P, 16 * S])
        context = big[:, 0:NT * D].rearrange("p (t d) -> p t d", t=NT)
        penalty = big[:, 0:KB * S].rearrange("p (k q) -> p k q", k=KB)
        penalty_raw = big[:, KB * S:2 * KB * S].rearrange("p (k q) -> p k q", k=KB)
        qst = sb("qst", [P, NG, HG * S], BF16)
        kst = sb("kst", [P, NG, HG * S], BF16)
        probs = sb("probs", [P, PRING, S])
        parts = sb("parts", [P, 6, S], BF16)
        qk_f = sb("qk_f", [P, 2, S])
        qk_r = sb("qk_r", [P, 2, S])
        vexp = sb("vexp", [P, NG, KB, HG, 32])
        vtok = sb("vtok", [P, KB, NH, HD])
        xb = sb("xb", [P, S])
        av_s = sb("av_s", [P, S])
        mx = sb("mx", [P, NG, UN])
        mrow = sb("mrow", [UN, NG, 2, P], BF16)
        wproj = sb("wproj", [P, 2, 3, D])
        wraw = big[:, 6144:6144 + 2 * 3 * D].rearrange("p (l t n) -> p l t n", l=2, t=3)
        wout = sb("wout", [P, D])
        bqk = sb("bqk", [P, 2, 2])
        bv = sb("bv", [P, 2, D])
        bo = sb("bo", [P, 1])
        ident = sb("ident", [P, P])
        ident16 = sb("ident16", [P, P], F16)
        mask_q = sb("mask_q", [P, P], F16)
        mask_k = sb("mask_k", [P, P], F16)
        ones = sb("ones", [P, P])
        dist = sb("dist", [P, 2 * S - P])
        disti = big[:, 7168:7168 + 2 * S - P].bitcast(mybir.dt.int32)
        w_raw = sb("w_raw", [P, 2, 2, F])
        stats = sb("stats", [P, NT, 6])
        lnw = sb("lnw", [P, 5, NT])
        pw = sb("pw", [P, 4, S])
        xn = probs[:, 0:NT * D // S, :].rearrange("p s (t d) -> p (s t) d", t=KB)
        xts = [[m.rearrange("p (t d) -> p t d", t=KB) for m in two]
               for two in ([pw[:, 2, :], pw[:, 3, :]], [big[:, 6656:7168], big[:, 7168:7680]])]
        xsplit = sb("xsplit", [P, 2, TOKENS], F16)
        w_split = big[:, 4096:6144].bitcast(F16).rearrange("p (s i f) -> p s i f", s=2, i=4)
        wgate = sb("wgate", [P, 2, E])
        bgate = sb("bgate", [P, E])
        eidx = sb("eidx", [P, E])
        eidx_i = sb("eidx_i", [P, E], mybir.dt.int32)
        gt = sb("gt", [P, 4, NT, E])
        gs = sb("gs", [P, 4, NT])
        cnt = sb("cnt", [P, E])
        ew = big[:, 4096:5120].rearrange("p (e d) -> p e d", e=E)
        ewT = big[:, 5120:6144].rearrange("p (e d) -> p e d", e=E)
        eb = sb("eb", [P, E])
        nb = sb("nb", [P, E])
        bsum = sb("bsum", [P, 1])
        rec = sb("rec", [P, KB, HG])
        ctx_t = sb("ctx_t", [P, KB, HG, HD])
        wg = sb("wg", [P, 1])
        bg = sb("bg", [P, 1])
        nbg = sb("nbg", [P, 1])
        zc = sb("zc", [P, 7, KB])
        lnbase = sb("lnbase", [P, 1])
        zrow = big[:, 6144:6144 + S]

        banks = [ctx.enter_context(nc.psum_tensor(f"bank{i}", [P, S], F32)) for i in range(8)]
        mxb, scb = (banks[0:2], banks[0:3]), (banks[2:5], banks[3:5])
        avb, m0 = banks[5:7], banks[7]
        logits, turned = banks[4], banks[5:7]
        scratch = nc.dram_tensor("qk_parts", [6, P, S], BF16, kind="Internal")

        d_x, d_w, d_out = sem("d_x"), sem("d_w"), sem("d_out")
        consts = sem("consts")
        cleared = sem("cleared")
        wready = sem("wready")
        ch = {n: sem(f"chain_{n}") for n in ("vector", "scalar", "gpsimd")}
        var_ok = [sem(f"var_ok{l}") for l in (0, 1)]
        std_ok = [sem(f"std_ok{l}") for l in (0, 1)]
        xn_ok = [sem(f"xn_ok{l}") for l in (0, 1)]
        tr_ok = [sem(f"tr_ok{l}") for l in (0, 1)]
        xts_ok = [sem(f"xts_ok{l}") for l in (0, 1)]
        xnT_ok = [sem(f"xnT_ok{l}") for l in (0, 1)]
        logits_ok = [sem(f"logits_ok{l}") for l in (0, 1)]
        gates_chain = sem("gates_chain")
        logits_out, g_sub, g_exp, mask_ok, cnt_ps, cnt_ok, ewT_ps, ewT_ok = (
            sem(n) for n in ("logits_out", "g_sub", "g_exp", "mask_ok", "cnt_ps", "cnt_ok", "ewT_ps", "ewT_ok"))
        A = []
        for l in (0, 1):
            names = ("stacked0 stacked1 stacked2 stacked3 shift0 shift1 shift2 shift3 spilled xb_ok "
                     "qk_ps q_used k_used hi_ok res_ok mid_ok lo_ok v_ps v_ok vexp_ok "
                     "mx_ps mx_ok mt_ps mhi_ok mrow_ok reach_ok sc_ps exp_ok pen_v pen_p av_ps "
                     "av_s_ok avt_ps norm_ok zc_ps ze_ok zc_ok zr_ps zr_ok penx_ok penq_ok "
                     "pent_ps penraw_ok pen_ok").split()
            A.append({n: sem(f"{n}_{l}") for n in names})
        ctile_ok, ct_ps, ctT_ok, op_ps, acc0_ok, ff_ps, acc_ok, yT_ps, x1_ok = (
            sem(n) for n in ("ctile_ok", "ct_ps", "ctT_ok", "op_ps", "acc0_ok", "ff_ps", "acc_ok", "yT_ps", "x1_ok"))
        w_in = [sem("w_in0"), sem("w_in1")]
        w_hi_ok, w_lo_ok, x_hi_ok, x_lo_ok = (sem(n) for n in ("w_hi_ok", "w_lo_ok", "x_hi_ok", "x_lo_ok"))
        up_ps, hid_ok, h_hi_ok, h_lo_ok, dn_ps, add_ok = (
            sem(n) for n in ("up_ps", "hid_ok", "h_hi_ok", "h_lo_ok", "dn_ps", "add_ok"))

        block = ctx.enter_context(nc.Block())

        def n_slot(u):
            return u % PRING

        def ring_bank(ring, g, u):
            return ring[(UN * g + u) % len(ring)]

        def ring_last(ring, g, u):
            i = UN * g + u
            return len(ring) if i >= len(ring) or len(ring) == 2 else (1, 4, 4)[i]

        def over_batches(eng, body):
            body(0, True, False)
            with eng.Fori(1, B - 1) as b:
                body(b, False, False)
            body(B - 1, False, True)

        def products(units, b, g, u):
            return sum(map(len, units)) * b + sum(map(len, units[:g])) + sum(v <= u for v in units[g])

        def unit_key(u):
            return u // HG, u % HG

        def unit_query(u):
            return u // KB, u % KB

        hidden = [probs[:, i * FC:(i + 1) * FC, :] for i in range(2)]
        h_split = [big[:, i * 2048:(i + 1) * 2048].bitcast(F16).rearrange("p (s c q) -> p s c q", s=2, c=FC)
                   for i in range(2)]

        @block.sync
        def _(sp):
            for c in range(4):
                sp.dma_start(x[:, c * 8:(c + 1) * 8, :],
                             io["x"].rearrange("b s d -> (b s) d").rearrange("(t p) d -> p t d", p=P)[:, c * 8:(c + 1) * 8, :]
                             ).then_inc(d_x, 16)

            def expert_load(e):
                if e >= 2:
                    sp.wait_ge(w_lo_ok, 2 * (e - 1))
                up = io["shared_up"][0] if e == 0 else io["routed_up"][e - 1]
                dn = io["shared_down"][0] if e == 0 else io["routed_down"][e - 1]
                sp.dma_start(w_raw[:, e % 2, 0, :], up).then_inc(w_in[e % 2], 16)
                sp.dma_start(w_raw[:, e % 2, 1, :].rearrange("p (c h) -> p c h", c=FC),
                             dn.rearrange("(c p) h -> p c h", p=P)).then_inc(w_in[e % 2], 16)

            for e in range(2):
                expert_load(e)
            sp.wait_ge(cleared, 3)
            for l in (0, 1):
                a = A[l]

                def spill(b):
                    if not (isinstance(b, int) and b == 0):
                        for g in range(NG):
                            sp.wait_ge(a[f"stacked{g}"], 96 * b)
                    sp.wait_ge(a["lo_ok"], 2 * b + 2)
                    sp.dma_start(scratch.ap().rearrange("s p q -> p s q"), parts[:, :, :]).then_inc(a["spilled"], 16)
                    sp.wait_ge(a["spilled"], 16 * b + 16)

                def stack(g):
                    for so in range(3):
                        rows = slice(24 * so, 24 * so + 24)
                        q_src = bass.AP(tensor=scratch.ap().tensor, offset=so * P * S + g * HG * S,
                                        ap=[[0, 3], [NH * S, HD], [1, HG * S]])
                        k_src = bass.AP(tensor=scratch.ap().tensor, offset=3 * P * S + g * HG * S,
                                        ap=[[P * S, 3], [NH * S, HD], [1, HG * S]])
                        sp.dma_start(qst[rows, g, :], q_src).then_inc(a[f"stacked{g}"], 16)
                        sp.dma_start(kst[rows, g, :], k_src).then_inc(a[f"stacked{g}"], 16)

                def shift(G, g):
                    sp.wait_ge(a["mrow_ok"], G + 1)
                    for r in range(2):
                        sp.dma_start(qst[SHIFT_ROW + r:SHIFT_ROW + r + 1, g, :], mrow[0:UN, g, r, :]
                                     ).then_inc(a[f"shift{g}"], 16)

                spill(0)
                for g in range(NG):
                    stack(g)
                shift(0, 0)

                def body(b, first, last):
                    for g in range(NG):
                        G = 4 * b + g
                        if not (first if g == 0 else last):
                            if g == 1:
                                spill(b + 1)
                            sp.wait_ge(a["sc_ps"], UN * G)
                            stack((g - 1) % NG)
                        if not (last and g == NG - 1):
                            shift(G + 1, (g + 1) % NG)

                over_batches(sp, body)
            for e in range(2, E + 1):
                expert_load(e)
            for b in range(B):
                sp.wait_ge(add_ok, 2 + B * E + b + 1)
                sp.dma_start(out[b].rearrange("(t p) d -> p t d", p=P), x[:, 4 * b:4 * b + 4, :]).then_inc(d_out, 16)
            sp.wait_ge(d_out, 16 * B)

        @block.gpsimd
        def _(pool):
            chain = Chain(pool, ch["gpsimd"])
            link = chain.link
            link(nc.gpsimd.memset(ident[:, :], 0.0))
            nc.gpsimd.affine_select(out=ident[:, :], in_=ident[:, :], compare_op=ALU.not_equal, fill=1.0,
                                    base=0, pattern=[[-1, P]], channel_multiplier=1).then_inc(consts, 1)
            link(nc.gpsimd.memset(ident16[:, :], 0.0))
            nc.gpsimd.affine_select(out=ident16[:, :], in_=ident16[:, :], compare_op=ALU.not_equal, fill=1.0,
                                    base=0, pattern=[[-1, P]], channel_multiplier=1).then_inc(consts, 1)
            link(nc.gpsimd.memset(mask_q[:, :], 0.0))
            nc.gpsimd.affine_select(out=mask_q[:, :], in_=mask_q[:, :], compare_op=ALU.is_ge, fill=-10000.0,
                                    base=0, pattern=[[-1, P]], channel_multiplier=1).then_inc(consts, 1)
            link(nc.gpsimd.memset(mask_k[:, :], 0.0))
            nc.gpsimd.affine_select(out=mask_k[:, :], in_=mask_k[:, :], compare_op=ALU.is_ge, fill=-10000.0,
                                    base=0, pattern=[[1, P]], channel_multiplier=-1).then_inc(consts, 1)
            nc.gpsimd.memset(ones[:, :], 1.0).then_inc(consts, 1)
            nc.gpsimd.memset(lnbase[:, :], float(np.log(S - 2.0))).then_inc(consts, 1)
            nc.gpsimd.iota(eidx_i[:, :], pattern=[[1, E]], base=-E, channel_multiplier=0).then_inc(consts, 1)
            nc.gpsimd.iota(disti[:, :], pattern=[[1, 2 * S - P]], base=-(S - P), channel_multiplier=-1).then_inc(consts, 1)
            pool.wait_ge(consts, 8)
            nc.gpsimd.memset(qst[64:SHIFT_ROW, :, :], 0.0).then_inc(cleared, 1)
            pool.wait_ge(cleared, 1)
            nc.gpsimd.memset(kst[64:SHIFT_ROW, :, :], 0.0).then_inc(cleared, 1)
            pool.wait_ge(cleared, 2)
            nc.gpsimd.memset(kst[SHIFT_ROW:SHIFT_ROW + 2, :, :], 1.0).then_inc(cleared, 1)
            pool.wait_ge(cleared, 3)
            link(nc.gpsimd.memset(vexp[:, :, :, :, HD + 1:32], 0.0))
            nc.gpsimd.memset(vexp[:, :, :, :, HD:HD + 1], 1.0).then_inc(cleared, 1)

            for b in range(B):
                cols = slice(b * S, (b + 1) * S)
                pool.wait_ge(xnT_ok[1], b + 1)
                pool.wait_ge(x_hi_ok, b + 1)
                nc.gpsimd.tensor_tensor(xsplit[:, 1, cols], xnT[:, cols], xsplit[:, 0, cols], ALU.subtract
                                        ).then_inc(x_lo_ok, 1)

            a = A[1]
            def body(b, first, last):
                for g in range(NG):
                    G = 4 * b + g
                    for u in range(UN):
                        if u in ON_POOL[g]:
                            kb = unit_key(u)[0]
                            n = UN * G + u
                            if g == 0:
                                pool.wait_ge(a["pen_ok"], KB * b + kb + 1)
                            pool.wait_ge(a["exp_ok"], n + 1)
                            t = probs[:, n_slot(u), :]
                            nc.gpsimd.tensor_tensor(t, t, penalty[:, kb, :], ALU.mult).then_inc(a["pen_p"], 1)

            over_batches(pool, body)

        @block.scalar
        def _(act):
            chain = Chain(act, ch["scalar"])
            link = chain.link
            with nc.allow_non_contiguous_dma(reason="small bias and gate loads"):
                loads = [
                    (wraw[:, 0, :, :], io["Wqkv"].rearrange("k (t n) -> k t n", t=3)),
                    (wraw[:, 1, 0, :], io["Wq"]), (wraw[:, 1, 1, :], io["Wk"]), (wraw[:, 1, 2, :], io["Wv"]),
                    (wout[:, :], io["Wout"]),
                    (ew[:, :, :], io["expert_w"].rearrange("e h d -> h e d")),
                    (wgate[:, 0, :], io["gate_w"].rearrange("e d -> d e")),
                    (wgate[:, 1, :], io["router_w"]),
                    (bgate[:, :], io["gate_b"].partition_broadcast(P)),
                    (eb[:, :], io["expert_b"].rearrange("e h -> h e")),
                    (bv[:, 0, :], io["bqkv"][2 * D:3 * D].partition_broadcast(P)),
                    (bv[:, 1, :], io["bv"].partition_broadcast(P)),
                    (bo[:, :], io["bout"].rearrange("(n o) -> n o", o=1)),
                    (wg[:, :], io["Wg"]),
                    (bg[:, :], io["bg"].partition_broadcast(P)),
                ]
                for l, t, v in ((0, 0, io["bqkv"][0:D]), (0, 1, io["bqkv"][D:2 * D]), (1, 0, io["bq"]), (1, 1, io["bk"])):
                    loads.append((bqk[:, l, t:t + 1],
                                  bass.AP(tensor=v.tensor, offset=v.offset, ap=[[1, HD], [HD, NH], [1, 1]])))
                for dst, src in loads:
                    act.dma_start(dst, src).then_inc(d_w, 16)
                assert len(loads) == LOADS

            def tiles_out(l, b):
                act.wait_ge(tr_ok[l], b + 1)
                if b >= 2:
                    act.wait_ge(xnT_ok[l], b - 1)
                    act.wait_ge(logits_ok[l], KB * (b - 1))
                bank = turned[b % 2]
                nc.scalar.activation(xts[l][b % 2], bank[:, :].rearrange("p (t d) -> p t d", t=KB), ACT.Copy
                                     ).then_inc(xts_ok[l], 1)
                if l == 1:
                    nc.scalar.activation(xsplit[:, 0, b * S:(b + 1) * S], bank[:, :], ACT.Copy).then_inc(x_hi_ok, 1)

            def attention_scalar(l):
                a = A[l]

                def prepare(b, what):
                    if what == "xb":
                        nc.scalar.activation(xb[:, :], xnT[:, bass.ds(b * S, S)], ACT.Copy).then_inc(a["xb_ok"], 1)
                        return
                    t = 0 if what[0] == "q" else 1
                    if what in ("q", "k"):
                        act.wait_ge(a["qk_ps"], 2 * b + t + 1)
                        nc.scalar.activation(qk_f[:, t, :], m0[:, :], ACT.Identity, bias=bqk[:, l, t:t + 1],
                                             scale=(1.0, HD ** -0.5)[t]).then_inc(a[what + "_used"], 1)
                    elif what in ("q_hi", "k_hi"):
                        act.wait_ge(a[what[0] + "_used"], b + 1)
                        nc.scalar.activation(parts[:, 3 * t, :], qk_f[:, t, :], ACT.Copy).then_inc(a["hi_ok"], 1)
                    elif what in ("q_mid", "k_mid"):
                        act.wait_ge(a["res_ok"], 2 * b + t + 1)
                        nc.scalar.activation(parts[:, 3 * t + 1, :], qk_r[:, t, :], ACT.Copy).then_inc(a["mid_ok"], 1)
                    elif what == "gate":
                        act.wait_ge(a["zc_ps"], b + 1)
                        nc.scalar.activation(zc[:, 0, :], m0[:, 0:KB], ACT.Exp, bias=nbg[:, :], scale=-1.0
                                             ).then_inc(a["ze_ok"], 1)
                    elif what == "reach":
                        act.wait_ge(a["zc_ok"], b + 1)
                        nc.scalar.activation(zc[:, 6, :], zc[:, 1, :], ACT.Exp, scale=-float(np.log(S - 2.0)),
                                             bias=lnbase[:, :]).then_inc(a["reach_ok"], 1)
                    elif what == "gates":
                        act.wait_ge(a["zr_ps"], b + 1)
                        nc.scalar.activation(zrow[:, :], m0[:, :], ACT.Copy).then_inc(a["zr_ok"], 1)
                    else:
                        i = int(what[-1])
                        n = KB * b + i
                        if what[:-1] == "u":
                            if i == 0:
                                act.wait_ge(a["zr_ok"], b + 1)
                            if not (isinstance(b, int) and n == 0):
                                act.wait_ge(a["penq_ok"], n)
                            nc.scalar.activation(pw[:, 0, :], zrow[:, :], ACT.Relu, scale=zc[:, 2, i:i + 1],
                                                 bias=zc[:, 3, i:i + 1])
                        elif what[:-1] == "t":
                            nc.scalar.activation(pw[:, 1, :], zrow[:, :], ACT.Relu, scale=zc[:, 5, i:i + 1],
                                                 bias=zc[:, 4, i:i + 1])
                        elif what[:-1] == "s":
                            if i == 0:
                                act.wait_ge(a["reach_ok"], b + 1)
                            lo = (KB - 1 - i) * P
                            nc.scalar.activation(pw[:, 2, :], dist[:, lo:lo + S], ACT.Identity,
                                                 bias=zc[:, 6, i:i + 1]).then_inc(a["penx_ok"], 1)
                        elif what[:-1] == "raw":
                            act.wait_ge(a["pent_ps"], n + 1)
                            if i == 0 and not (isinstance(b, int) and b == 0):
                                act.wait_ge(a["pen_ok"], KB * b)
                            nc.scalar.activation(penalty_raw[:, :, i * P:(i + 1) * P],
                                                 m0[:, :].rearrange("p (k q) -> p k q", k=KB), ACT.Copy
                                                 ).then_inc(a["penraw_ok"], 1)

                def put_v(g):
                    nc.scalar.activation(vexp[:, g, :, :, 0:HD], vtok[:, :, HG * g:HG * g + HG, :], ACT.Copy
                                         ).then_inc(a["vexp_ok"], 1)

                def shift_hi(G, g):
                    act.wait_ge(a["mt_ps"], G + 1)
                    nc.scalar.activation(mrow[:, g, 0, :], m0[0:UN, 0:P], ACT.Copy, scale=-1.0).then_inc(a["mhi_ok"], 1)

                act.wait_ge(var_ok[l], 1)
                nc.scalar.activation(lnw[:, 4, :], lnw[:, 3, :], ACT.Sqrt).then_inc(std_ok[l], 1)
                tiles_out(l, 0)
                act.wait_ge(xnT_ok[l], 1)
                for what in ("xb", "q", "q_hi", "k", "k_hi", "q_mid", "k_mid"):
                    prepare(0, what)
                if l == 1:
                    for what in ("gate", "reach", "gates", "u0", "t0", "s0"):
                        prepare(0, what)
                act.wait_ge(a["v_ok"], 1)
                act.wait_ge(cleared, 4)
                for g in range(NG):
                    put_v(g)
                for b in range(1, EARLY + 1):
                    tiles_out(l, b)
                for i in range(KB):
                    if EARLY + 1 + i < B:
                        tiles_out(l, EARLY + 1 + i)
                    if l == 1:
                        prepare(0, f"raw{i}")
                        if i + 1 < KB:
                            for what in "uts":
                                prepare(0, f"{what}{i + 1}")
                act.wait_ge(xnT_ok[l], B)
                act.wait_ge(logits_ok[l], NT)
                shift_hi(0, 0)
                lag = LAG[l]

                def gates(what):
                    if what == "exponentials":
                        act.wait_ge(g_sub, 1)
                        nc.scalar.activation(gt[:, 1, :, :], gt[:, 1, :, :], ACT.Exp).then_inc(g_exp, 1)
                    else:
                        half = int(what[-1])
                        act.wait_ge(ewT_ps, half + 1)
                        act.wait_ge(cnt_ok, 1)
                        for i in range(4):
                            e = 4 * half + i
                            nc.scalar.activation(ewT[:, e, :], m0[:, i * P:(i + 1) * P], ACT.Copy,
                                                 scale=cnt[:, e:e + 1]).then_inc(ewT_ok, 1)

                def tail(G, g):
                    act.wait_ge(a["av_ps"], UN * G)
                    if not isinstance(G, int) or G >= 2:
                        act.wait_ge(a["avt_ps"], G - 1)
                    nc.scalar.activation(av_s[:, :], avb[g % 2][:, :], ACT.Copy).then_inc(a["av_s_ok"], 1)

                def body(b, first, last):
                    for g in range(NG):
                        G = 4 * b + g
                        for u in range(UN):
                            n = UN * G + u
                            act.wait_ge(a["sc_ps"], n + 1)
                            if not first or UN * g + u >= PRING:
                                act.wait_ge(a["av_ps"], n - PRING + 1)
                            lo = unit_key(u)[0] * P if l == 0 else 0
                            nc.scalar.activation(probs[:, n_slot(u), lo:S], ring_bank(scb[l], g, u)[:, 0:S - lo], ACT.Exp
                                                 ).then_inc(a["exp_ok"], 1)
                            if u == SHIFT[l][0] and not (last and g == NG - 1):
                                shift_hi(G + 1, (g + 1) % NG)
                            if u == lag + 1 and not (first and g == 0):
                                tail(G, (g - 1) % NG)
                            if u == lag + 2 and not (first if g == 0 else last):
                                act.wait_ge(a["v_ok"], (b if g == 0 else b + 1) + 1)
                                put_v((g - 1) % NG)
                            if last:
                                if (g, u) in SCALAR_LAST[l]:
                                    gates(SCALAR_LAST[l][g, u])
                                continue
                            what = SCALAR_NEXT[l].get((g, u))
                            if what == "xb":
                                act.wait_ge(a["v_ps"], b + 1)
                                if l == 1:
                                    act.wait_ge(a["zc_ps"], b + 1)
                            if what == "q_hi":
                                act.wait_ge(a["spilled"], 16 * (b + 1))
                            if what:
                                prepare(b + 1, what)

                over_batches(act, body)
                tail(B * NG, (NG - 1) % NG)

            attention_scalar(0)

            def out_scalar(b, half):
                act.wait_ge(ct_ps, b + 1)
                nc.scalar.activation(av_s[:, :], m0[:, :], ACT.Copy).then_inc(ctT_ok, 1)
                act.wait_ge(op_ps, b + 1)
                nc.scalar.activation(qk_f[:, half, :], banks[6][:, :], ACT.Identity, bias=bsum[:, :]).then_inc(acc0_ok, 1)

            with act.Fori(0, B // 2) as t:
                for half in range(2):
                    out_scalar(2 * t + half, half)

            def weights_hi(e):
                act.wait_ge(w_in[e % 2], 32 * (e // 2 + 1))
                if e >= 2:
                    act.wait_ge(dn_ps, B * (e - 1))
                for i in range(2):
                    nc.scalar.activation(w_split[:, e % 2, 2 * i, :], w_raw[:, e % 2, i, :], ACT.Copy, scale=W_SCALE
                                         ).then_inc(w_hi_ok, 1)

            act.wait_ge(yT_ps, B)
            weights_hi(0)
            attention_scalar(1)

            def experts_pair(e, t, first):
                for half in range(2):
                    n = B * e + 2 * t + half
                    for c in range(FC):
                        act.wait_ge(up_ps, FC * n + c + 1)
                        if c == 0 and not first:
                            act.wait_ge(dn_ps, n - 1)
                        nc.scalar.activation(hidden[half][:, c, :], banks[c][:, :], ACT.Gelu, scale=1.0 / W_SCALE
                                             ).then_inc(hid_ok, 1)
                        act.wait_ge(hid_ok, FC * n + c + 1)
                        nc.scalar.activation(h_split[half][:, 0, c, :], hidden[half][:, c, :], ACT.Copy,
                                             scale=H_SCALE).then_inc(h_hi_ok, 1)

            for e in range(E + 1):
                experts_pair(e, 0, e == 0)
                if e < E:
                    weights_hi(e + 1)
                with act.Fori(1, B // 2) as t:
                    experts_pair(e, t, False)

        @block.vector
        def _(dve):
            chain = Chain(dve, ch["vector"])
            link = chain.link
            vec = nc.vector

            def statistics(l, meanwhile):
                for t in range(NT):
                    last = vec.bn_stats(stats[:, t, :], x[:, t, :])
                link(last)
                me, qe, mo, qo = (stats[:, :, i] for i in (1, 2, 4, 5))
                mean, dif, var, std = lnw[:, 0, :], lnw[:, 1, :], lnw[:, 3, :], lnw[:, 4, :]
                link(vec.tensor_tensor(mean, me, mo, ALU.add))
                link(vec.tensor_scalar(mean, mean, 0.5, None, ALU.mult))
                link(vec.tensor_tensor(dif, me, mo, ALU.subtract))
                link(vec.tensor_tensor(dif, dif, dif, ALU.mult))
                link(vec.tensor_tensor(var, qe, qo, ALU.add))
                link(vec.tensor_scalar(var, var, 1.0 / D, EPS, ALU.mult, ALU.add))
                vec.scalar_tensor_tensor(var, dif, 0.25, var, ALU.mult, ALU.add).then_inc(var_ok[l], 1)
                meanwhile()
                dve.wait_ge(std_ok[l], 1)
                link(vec.reciprocal(lnw[:, 2, :], std))

            def tiles_in(l, b):
                for t in range(KB * b, KB * b + KB):
                    last = vec.tensor_scalar(xn[:, t, :], x[:, t, :], lnw[:, 0, t:t + 1], lnw[:, 2, t:t + 1],
                                             ALU.subtract, ALU.mult)
                last.then_inc(xn_ok[l], 1)

            def activations(l, b):
                if l == 1:
                    dve.wait_ge(xn_ok[l], b + 1)
                    dst = x[:, KB * b:KB * b + KB, :]
                    vec.tensor_tensor(dst, dst, xn[:, KB * b:KB * b + KB, :], ALU.add)
                dve.wait_ge(xts_ok[l], b + 1)
                vec.tensor_copy(xnT[:, b * S:(b + 1) * S], xts[l][b % 2].rearrange("p t d -> p (t d)")
                                ).then_inc(xnT_ok[l], 1)

            wide = lambda v: v.unsqueeze(2).broadcast_to((P, NT, E))
            gating = Chain(dve, gates_chain)

            def onehot(src, dst, tmp):
                best, at = gs[:, 2, :], gs[:, 3, :]
                idx = eidx[:, :].unsqueeze(1).broadcast_to((P, NT, E))
                gating.link(vec.reduce_max(best, src, AX.X))
                gating.link(vec.tensor_tensor(tmp, src, wide(best), ALU.is_equal))
                gating.link(vec.tensor_tensor(tmp, tmp, idx, ALU.mult))
                gating.link(vec.tensor_reduce(at, tmp, AX.X, ALU.min))
                gating.link(vec.tensor_tensor(dst, idx, wide(at), ALU.is_equal))

            def gates(l, what):
                g, rest, hot, hot2 = gt[:, l, :, :], gt[:, 1 - l, :, :], gt[:, 2, :, :], gt[:, 3, :, :]
                if what == "logits":
                    dve.wait_ge(logits_ok[l], NT)
                    src = logits[:, 0:NT * E].rearrange("p (t e) -> p t e", e=E)
                    if l == 0:
                        gb = bgate[:, :].unsqueeze(1).broadcast_to((P, NT, E))
                        vec.tensor_tensor(gt[:, 0, :, :], src, gb, ALU.add).then_inc(logits_out, 1)
                    else:
                        vec.tensor_copy(gt[:, 0, :, :], src).then_inc(logits_out, 1)
                elif what == "shifted":
                    gating.link(vec.reduce_max(gs[:, 0, :], gt[:, 0, :, :], AX.X))
                    vec.tensor_tensor(gt[:, 1, :, :], gt[:, 0, :, :], wide(gs[:, 0, :]), ALU.subtract).then_inc(g_sub, 1)
                elif what == "softmax":
                    dve.wait_ge(g_exp, 1)
                    gating.link(vec.reduce_sum(gs[:, 0, :], gt[:, 1, :, :], AX.X))
                    gating.link(vec.reciprocal(gs[:, 1, :], gs[:, 0, :]))
                    gating.link(vec.tensor_tensor(gt[:, 1, :, :], gt[:, 1, :, :], wide(gs[:, 1, :]), ALU.mult))
                elif what == "best":
                    if l == 0:
                        dve.wait_ge(logits_out, 1)
                        dve.wait_ge(consts, 10)
                    onehot(g, hot, hot2)
                elif what == "second":
                    gating.link(vec.scalar_tensor_tensor(rest, hot, -3.0e38, g, ALU.mult, ALU.add))
                    onehot(rest, hot2, hot2)
                elif what == "mask":
                    vec.tensor_tensor(gt[:, 0, :, :], hot, hot2, ALU.add).then_inc(mask_ok, 1)
                elif what == "shares":
                    dve.wait_ge(cnt_ps, 1)
                    src = m0[:, 0:NT * E].rearrange("p (t e) -> p e t", e=E)
                    gating.link(vec.reduce_sum(cnt[:, :], src, AX.X))
                    gating.link(vec.tensor_scalar(cnt[:, :], cnt[:, :], 1.0 / (2 * TOKENS), None, ALU.mult))
                    gating.link(vec.scalar_tensor_tensor(nb[:, :], cnt[:, :], -1.0, eb[:, :], ALU.mult, ALU.mult))
                    gating.link(vec.reduce_sum(bsum[:, :], nb[:, :], AX.X))
                    vec.tensor_tensor(bsum[:, :], bo[:, :], bsum[:, :], ALU.subtract).then_inc(cnt_ok, 1)
                elif what == "gates":
                    gating.link(vec.tensor_tensor(hot, hot, hot2, ALU.add))
                    gating.link(vec.scalar_tensor_tensor(hot, hot, 1.0 / (W_SCALE * H_SCALE), g, ALU.mult, ALU.mult))

            def attention_vector(l):
                a = A[l]
                lag = LAG[l]

                def prepare(b, what):
                    t = 0 if what[0] == "q" else 1
                    if what in ("q_res", "k_res"):
                        dve.wait_ge(a["hi_ok"], 2 * b + t + 1)
                        vec.tensor_tensor(qk_r[:, t, :], qk_f[:, t, :], parts[:, 3 * t, :], ALU.subtract
                                          ).then_inc(a["res_ok"], 1)
                    elif what in ("q_lo", "k_lo"):
                        dve.wait_ge(a["mid_ok"], 2 * b + t + 1)
                        vec.tensor_tensor(parts[:, 3 * t + 2, :], qk_r[:, t, :], parts[:, 3 * t + 1, :], ALU.subtract
                                          ).then_inc(a["lo_ok"], 1)
                    elif what == "v":
                        dve.wait_ge(a["v_ps"], b + 1)
                        bias = bv[:, l, :].unsqueeze(1).broadcast_to((P, KB, D))
                        vec.tensor_tensor(vtok[:, :, :, :].rearrange("p k h d -> p k (h d)"),
                                          m0[:, :].rearrange("p (k n) -> p k n", k=KB), bias, ALU.add
                                          ).then_inc(a["v_ok"], 1)
                    elif what == "gate":
                        dve.wait_ge(a["ze_ok"], b + 1)
                        link(vec.tensor_scalar(zc[:, 0, :], zc[:, 0, :], 1.0, None, ALU.add))
                        link(vec.reciprocal(zc[:, 1, :], zc[:, 0, :]))
                        link(vec.tensor_scalar(zc[:, 2, :], zc[:, 1, :], -1.0, None, ALU.add))
                        vec.tensor_tensor(zc[:, 3, :], zc[:, 2, :], zc[:, 2, :], ALU.mult)
                        vec.tensor_tensor(zc[:, 4, :], zc[:, 1, :], zc[:, 1, :], ALU.mult)
                        vec.tensor_scalar(zc[:, 5, :], zc[:, 1, :], -1.0, None, ALU.mult).then_inc(a["zc_ok"], 1)
                    elif what[:-1] == "sum":
                        i = int(what[-1])
                        dve.wait_ge(a["penx_ok"], KB * b + i + 1)
                        link(vec.scalar_tensor_tensor(pw[:, 0, :], pw[:, 0, :], zc[:, 1, i:i + 1], pw[:, 1, :],
                                                      ALU.add, ALU.subtract))
                    elif what[:-1] == "product":
                        i = int(what[-1])
                        n = KB * b + i
                        if not (isinstance(b, int) and n == 0):
                            dve.wait_ge(a["pent_ps"], n)
                        vec.scalar_tensor_tensor(pw[:, 3, :], pw[:, 2, :], 1.0, pw[:, 0, :], ALU.min, ALU.mult
                                                 ).then_inc(a["penq_ok"], 1)
                    elif what[:-1] == "put":
                        kb = int(what[-1])
                        if kb == 0:
                            dve.wait_ge(a["penraw_ok"], KB * b + KB)
                        if not (isinstance(b, int) and b == 0):
                            dve.wait_ge(a["pen_p"], products(ON_POOL, b - 1, NG - 1, HG * kb + HG - 1))
                        vec.tensor_scalar(penalty[:, kb, :], penalty_raw[:, kb, :], 1e-32, None, ALU.max
                                          ).then_inc(a["pen_ok"], 1)

                def maxima(n, G, g, u):
                    j, qb = unit_query(u)
                    width = (qb + 1) * P if l == 0 else S
                    dve.wait_ge(a["mx_ps"], n + 1)
                    vec.reduce_max(mx[:, g, u:u + 1], ring_bank(mxb[l], g, u)[:, 0:width], AX.X).then_inc(a["mx_ok"], 1)

                def shift_mid(G, g):
                    dve.wait_ge(a["mhi_ok"], G + 1)
                    vec.scalar_tensor_tensor(mrow[:, g, 1, :], m0[0:UN, 0:P], -1.0, mrow[:, g, 0, :],
                                             ALU.mult, ALU.subtract).then_inc(a["mrow_ok"], 1)

                def tail(G, g):
                    dve.wait_ge(a["avt_ps"], G)
                    ps = m0[:, :].rearrange("p (q j c) -> p q j c", q=KB, j=HG)
                    link(vec.reciprocal(rec[:, :, :], ps[:, :, :, HD]))
                    ratio = rec[:, :, :].unsqueeze(3).broadcast_to((P, KB, HG, HD))
                    return ps, ratio

                def tail_to(G, g, bt):
                    ps, ratio = tail(G, g)
                    cols = slice(g * HG * HD, (g + 1) * HG * HD)
                    if l == 0:
                        dst = context[:, bass.ds(bt * KB, KB), cols].rearrange("p q (j d) -> p q j d", j=HG)
                        vec.tensor_tensor(dst, ps[:, :, :, 0:HD], ratio, ALU.mult).then_inc(a["norm_ok"], 1)
                    else:
                        link(vec.tensor_tensor(ctx_t[:, :, :, :], ps[:, :, :, 0:HD], ratio, ALU.mult))
                        dst = x[:, bass.ds(bt * KB, KB), cols]
                        vec.tensor_tensor(dst, dst, ctx_t[:, :, :, :].rearrange("p q j d -> p q (j d)"), ALU.add
                                          ).then_inc(a["norm_ok"], 1)

                for b in range(4):
                    tiles_in(l, b)
                activations(l, 0)
                for b in range(4, B):
                    tiles_in(l, b)
                for what in ("q_res", "k_res", "q_lo", "k_lo", "v"):
                    prepare(0, what)
                if l == 1:
                    prepare(0, "gate")
                    prepare(0, "sum0")
                    prepare(0, "product0")
                    weights_lo(0)
                for b in range(1, EARLY + 1):
                    activations(l, b)
                for G in range(2):
                    for u in range(UN):
                        n = UN * G + u
                        maxima(n, G, G, u)
                        if n % 8 == 3 and EARLY + 1 + n // 8 < B:
                            activations(l, EARLY + 1 + n // 8)
                        if l == 1 and n % 8 == 1 and n > 8:
                            prepare(0, f"sum{n // 8}")
                            prepare(0, f"product{n // 8}")
                gates(l, "logits")
                if l == 1:
                    for kb in range(KB):
                        prepare(0, f"put{kb}")
                shift_mid(0, 0)
                start = chain.base + chain.k
                per = NG if l == 0 else 2 * NG + 3 + KB

                def body(b, first, last):
                    chain.start(start + per * b)
                    for g in range(NG):
                        G = 4 * b + g
                        for u in range(UN):
                            if not (last and g >= 2):
                                if u == 0 and not (first and g < 2):
                                    dve.wait_ge(a["mt_ps"], G - 1)
                                maxima(UN * (G + 2) + u, G + 2, (g + 2) % NG, u)
                            if l == 1:
                                v = u - 1
                                if v in ON_DVE[g]:
                                    dve.wait_ge(a["exp_ok"], UN * G + v + 1)
                                    t = probs[:, n_slot(v), :]
                                    vec.tensor_tensor(t, t, penalty[:, unit_key(v)[0], :], ALU.mult
                                                      ).then_inc(a["pen_v"], 1)
                            if l == 1 and g == 0 and 0 < u < KB and not first:
                                prepare(b, f"put{u}")
                            if u == SHIFT[l][1] and not (last and g == NG - 1):
                                shift_mid(G + 1, (g + 1) % NG)
                            if u == NORM[l] and not (first and g == 0):
                                tail_to(G, (g - 1) % NG, b if g else b - 1)
                            if last:
                                if (g, u) in VECTOR_LAST[l]:
                                    gates(l, VECTOR_LAST[l][g, u])
                                continue
                            what = VECTOR_NEXT[l].get((g, u))
                            if what == "v":
                                dve.wait_ge(a["vexp_ok"], NG * b + NG)
                            if what:
                                prepare(b + 1, what)
                    chain.fill(per)

                over_batches(dve, body)
                chain.start(start + per * B)
                tail_to(B * NG, NG - 1, B - 1)

            dve.wait_ge(consts, 8)
            vec.tensor_copy(eidx[:, :], eidx_i[:, :]).then_inc(consts, 1)
            link(vec.tensor_copy(dist[:, :], disti[:, :]))
            link(vec.scalar_tensor_tensor(dist[:, :], dist[:, :], -1.0, dist[:, :], ALU.mult, ALU.max))
            vec.tensor_scalar(dist[:, :], dist[:, :], -1.0, 2.0, ALU.mult, ALU.add).then_inc(consts, 1)
            dve.wait_ge(d_x, 64)
            def arrange_weights():
                dve.wait_ge(d_w, 16 * LOADS)
                for l in (0, 1):
                    for t in range(2):
                        vec.tensor_copy(wproj[:, l, t, :].rearrange("p (d h) -> p d h", d=HD),
                                        wraw[:, l, t, :].rearrange("p (h d) -> p d h", d=HD)).then_inc(wready, 1)
                    vec.tensor_copy(wproj[:, l, 2, :], wraw[:, l, 2, :]).then_inc(wready, 1)
                    vec.tensor_scalar(bqk[:, l, 1:2], bqk[:, l, 1:2], HD ** -0.5, None, ALU.mult).then_inc(wready, 1)
                vec.tensor_scalar(nbg[:, :], bg[:, :], -1.0, None, ALU.mult).then_inc(wready, 1)

            statistics(0, arrange_weights)
            attention_vector(0)

            dve.wait_ge(A[0]["norm_ok"], B * NG)

            def contexts_out(b, half):
                if not (isinstance(b, int) and b < 2):
                    dve.wait_ge(ct_ps, b - 1)
                vec.tensor_copy(xts[0][half], context[:, bass.ds(b * KB, KB), :]).then_inc(ctile_ok, 1)

            def stream_add(b):
                dve.wait_ge(yT_ps, b + 1)
                dst = x[:, bass.ds(b * KB, KB), :]
                vec.tensor_tensor(dst, dst, banks[4][:, :].rearrange("p (t d) -> p t d", t=KB), ALU.add
                                  ).then_inc(x1_ok, 1)

            def out_pair(t, first, last):
                for half in range(2):
                    b = 2 * t + half
                    if not (last and half == 1):
                        contexts_out(b + 1, 1 - half)
                    dve.wait_ge(acc0_ok, b + 1)
                    acc = qk_f[:, half, :]
                    for e in range(E):
                        dve.wait_ge(ff_ps, E * b + e + 1)
                        vec.scalar_tensor_tensor(acc, banks[e % 4][:, :], nb[:, e:e + 1], acc, ALU.max, ALU.add
                                                 ).then_inc(acc_ok, 1)
                        if e == 3 and not (first and half == 0):
                            stream_add(b - 1)
                        dve.wait_ge(acc_ok, E * b + e + 1)

            contexts_out(0, 0)
            out_pair(0, True, False)
            with dve.Fori(1, B // 2 - 1) as t:
                out_pair(t, False, False)
            out_pair(B // 2 - 1, False, True)
            stream_add(B - 1)
            dve.wait_ge(x1_ok, B)

            def weights_lo(e):
                for i in range(2):
                    dve.wait_ge(w_hi_ok, 2 * e + i + 1)
                    vec.scalar_tensor_tensor(w_split[:, e % 2, 2 * i + 1, :], w_raw[:, e % 2, i, :], W_SCALE,
                                             w_split[:, e % 2, 2 * i, :], ALU.mult, ALU.subtract).then_inc(w_lo_ok, 1)

            statistics(1, lambda: None)
            attention_vector(1)
            dve.wait_ge(A[1]["norm_ok"], B * NG)

            dve.sem_inc(add_ok, 2)

            def halves_lo(n, half):
                for c in range(FC):
                    dve.wait_ge(h_hi_ok, FC * n + c + 1)
                    vec.scalar_tensor_tensor(h_split[half][:, 1, c, :], hidden[half][:, c, :], H_SCALE,
                                             h_split[half][:, 0, c, :], ALU.mult, ALU.subtract).then_inc(h_lo_ok, 1)

            def expert_add(e, n, b, half):
                dve.wait_ge(dn_ps, n + 1)
                for i in range(KB):
                    t = KB * b + i
                    src = banks[4 + half][:, i * P:(i + 1) * P]
                    gate = 1.0 / (W_SCALE * H_SCALE) if e == 0 else gt[:, 2, t, e - 1:e]
                    ins = vec.scalar_tensor_tensor(x[:, t, :], src, gate, x[:, t, :], ALU.mult, ALU.add)
                ins.then_inc(add_ok, 1)

            for e in range(E + 1):
                n = B * e
                halves_lo(n, 0)
                if e > 0:
                    expert_add(e - 1, n - 1, B - 1, 1)
                    dve.wait_ge(add_ok, 2 + n)
                halves_lo(n + 1, 1)
                if e < E:
                    weights_lo(e + 1)
                expert_add(e, n, 0, 0)
                with dve.Fori(1, B // 2) as t:
                    for half in range(2):
                        halves_lo(n + 2 * t + half, half)
                        expert_add(e, n + 2 * t + half - 1, 2 * t + half - 1, 1 - half)
            expert_add(E, B * E + B - 1, B - 1, 1)

        @block.tensor
        def _(pe):
            mm = nc.tensor.matmul
            transpose = nc.tensor.transpose

            def turn_tiles(l, b):
                pe.wait_ge(xn_ok[l], b + 1)
                if b >= 2:
                    pe.wait_ge(xts_ok[l], b - 1)
                    if l == 1:
                        pe.wait_ge(x_hi_ok, b - 1)
                for i in range(KB):
                    last = transpose(turned[b % 2][:, i * P:(i + 1) * P], xn[:, KB * b + i, :], ident[:, :])
                last.then_inc(tr_ok[l], 1)

            def gate_logits(l, b):
                pe.wait_ge(xts_ok[l], b + 1)
                for i in range(KB):
                    t8 = (KB * b + i) * E
                    mm(logits[:, t8:t8 + E], xts[l][b % 2][:, i, :], wgate[:, l, :],
                       start=True, stop=True).then_inc(logits_ok[l], 1)

            def attention_tensor(l):
                a = A[l]
                lag = LAG[l]

                spare_last = [None]

                def spare(what, b):
                    if spare_last[0] is not None:
                        pe.wait_ge(*spare_last[0])
                    if what == "q":
                        pe.wait_ge(a["xb_ok"], b + 1)
                    if what in ("q", "k"):
                        t = 0 if what == "q" else 1
                        mm(m0[:, :], wproj[:, l, t, :], xb[:, :], start=True, stop=True).then_inc(a["qk_ps"], 1)
                        spare_last[0] = (a[what + "_used"], b + 1)
                    elif what == "v":
                        for kb in range(KB):
                            last = mm(m0[:, kb * P:(kb + 1) * P], xb[:, kb * P:(kb + 1) * P], wproj[:, l, 2, :],
                                      start=True, stop=True)
                        last.then_inc(a["v_ps"], 1)
                        spare_last[0] = (a["v_ok"], b + 1)
                    elif what == "gate":
                        for kb in range(KB):
                            last = mm(m0[:, kb:kb + 1], xb[:, kb * P:(kb + 1) * P], wg[:, :], start=True, stop=True)
                        last.then_inc(a["zc_ps"], 1)
                        spare_last[0] = (a["ze_ok"], b + 1)
                    elif what == "gates":
                        pe.wait_ge(a["zc_ok"], b + 1)
                        for kb in range(KB):
                            last = mm(m0[:, kb * P:(kb + 1) * P], zc[:, 1, kb:kb + 1].broadcast_to((P, P)),
                                      ident[:, :], start=True, stop=True)
                        last.then_inc(a["zr_ps"], 1)
                        spare_last[0] = (a["zr_ok"], b + 1)
                    elif what.startswith("penalty"):
                        i = int(what[-1])
                        pe.wait_ge(a["penq_ok"], KB * b + i + 1)
                        for kb in range(KB):
                            last = transpose(m0[:, kb * P:(kb + 1) * P], pw[:, 3, kb * P:(kb + 1) * P], ident[:, :])
                        last.then_inc(a["pent_ps"], 1)
                        spare_last[0] = (a["penraw_ok"], KB * b + i + 1)
                    elif what == "counts":
                        pe.wait_ge(mask_ok, 1)
                        mm(m0[:, 0:NT * E], ones[:, :], gt[:, 0, :, :].rearrange("p t e -> p (t e)"),
                           start=True, stop=True).then_inc(cnt_ps, 1)
                        spare_last[0] = (cnt_ok, 1)
                    elif what.startswith("weights"):
                        half = int(what[-1])
                        for i in range(4):
                            last = transpose(m0[:, i * P:(i + 1) * P], ew[:, 4 * half + i, :], ident[:, :])
                        last.then_inc(ewT_ps, 1)
                        spare_last[0] = (ewT_ok, 4 * (half + 1))

                def turn_maxima(G, g):
                    if spare_last[0] is not None:
                        pe.wait_ge(*spare_last[0])
                    pe.wait_ge(a["mx_ok"], UN * (G + 1))
                    transpose(m0[0:UN, 0:P], mx[:, g, :], ident[:, :]).then_inc(a["mt_ps"], 1)
                    spare_last[0] = (a["mrow_ok"], G + 1)

                def turn_context(G):
                    if spare_last[0] is not None:
                        pe.wait_ge(*spare_last[0])
                    pe.wait_ge(a["av_s_ok"], G)
                    for qb in range(KB):
                        last = transpose(m0[:, qb * P:(qb + 1) * P], av_s[:, qb * P:(qb + 1) * P], ident[:, :])
                    last.then_inc(a["avt_ps"], 1)
                    spare_last[0] = (a["norm_ok"], G)

                def score_max(n, g, u, free):
                    j, qb = unit_query(u)
                    bank = ring_bank(mxb[l], g, u)
                    if free is not None:
                        pe.wait_ge(a["mx_ok"], free)
                    lhs = qst[0:SHIFT_ROW, g, j * S + qb * P:j * S + (qb + 1) * P]
                    if l == 0:
                        mm(bank[:, 0:(qb + 1) * P], lhs, kst[0:SHIFT_ROW, g, j * S:j * S + (qb + 1) * P],
                           start=True, stop=False)
                        mm(bank[:, qb * P:(qb + 1) * P], ident16[:, :], mask_q[:, :], start=False, stop=True
                           ).then_inc(a["mx_ps"], 1)
                    else:
                        mm(bank[:, :], lhs, kst[0:SHIFT_ROW, g, j * S:(j + 1) * S], start=True, stop=True
                           ).then_inc(a["mx_ps"], 1)

                def score(n, g, u, free):
                    kb, j = unit_key(u)
                    bank = ring_bank(scb[l], g, u)
                    if free is not None:
                        pe.wait_ge(a["exp_ok"], free)
                    rows = slice(0, SHIFT_ROW + 2)
                    lhs = kst[rows, g, j * S + kb * P:j * S + (kb + 1) * P]
                    if l == 0:
                        mm(bank[:, 0:S - kb * P], lhs, qst[rows, g, j * S + kb * P:(j + 1) * S], start=True, stop=False)
                        mm(bank[:, 0:P], ident16[:, :], mask_k[:, :], start=False, stop=True).then_inc(a["sc_ps"], 1)
                    else:
                        mm(bank[:, :], lhs, qst[rows, g, j * S:(j + 1) * S], start=True, stop=True).then_inc(a["sc_ps"], 1)

                def weigh(n, b, g, u):
                    kb, j = unit_key(u)
                    if l == 0:
                        pe.wait_ge(a["exp_ok"], n + 1)
                    elif u in ON_DVE[g]:
                        pe.wait_ge(a["pen_v"], products(ON_DVE, b, g, u))
                    else:
                        pe.wait_ge(a["pen_p"], products(ON_POOL, b, g, u))
                    lo = kb * P if l == 0 else 0
                    last = mm(avb[g % 2][32 * j:32 * j + 32, lo:S], vexp[:, g, kb, j, :], probs[:, n_slot(u), lo:S],
                              start=(kb == 0), stop=(kb == KB - 1))
                    last.then_inc(a["av_ps"], 1)

                turn_tiles(l, 0)
                pe.wait_ge(wready, 9)
                for what in ("q", "k", "v") if l == 0 else ("q", "k", "v", "gate", "gates"):
                    spare(what, 0)
                for b in range(1, EARLY + 1):
                    turn_tiles(l, b)
                    gate_logits(l, b - 1)
                for G in range(2):
                    pe.wait_ge(a[f"stacked{G}"], 6 * 16)
                    for u in range(UN):
                        n = UN * G + u
                        score_max(n, G, u, n - ring_last(mxb[l], G, u) + 1 if n >= len(mxb[l]) else None)
                        if n % 8 == 3:
                            b = EARLY + 1 + n // 8
                            if b < B:
                                turn_tiles(l, b)
                            gate_logits(l, b - 1)
                        if l == 1 and n % 8 == 5:
                            spare(f"penalty{n // 8}", 0)
                pe.wait_ge(logits_out, l + 1)
                turn_maxima(0, 0)

                def body(b, first, last):
                    if not first:
                        spare_last[0] = (a["norm_ok"], NG * b - 1) if l == 0 else (a["penraw_ok"], KB * (b + 1))
                    for g in range(NG):
                        G = 4 * b + g
                        for u in range(UN):
                            if not (last and g >= 2):
                                g2, n2 = (g + 2) % NG, UN * (G + 2) + u
                                if u == 0:
                                    pe.wait_ge(a[f"stacked{g2}"], 6 * 16 * ((b if g < 2 else b + 1) + 1))
                                score_max(n2, g2, u, n2 - ring_last(mxb[l], g2, u) + 1)
                            if u == 0:
                                pe.wait_ge(a[f"shift{g}"], 32 * (b + 1))
                            n = UN * G + u
                            score(n, g, u, None if first and UN * g + u < len(scb[l]) else n - ring_last(scb[l], g, u) + 1)
                            if u >= lag:
                                if u == lag and not (first and g < 1):
                                    if not (first and g < 2):
                                        pe.wait_ge(a["av_s_ok"], G - 1)
                                if u == lag:
                                    pe.wait_ge(a["vexp_ok"], vexp_needed(b, g, first))
                                weigh(n - lag, b, g, u - lag)
                            elif not (first and g == 0):
                                weigh(n - lag, b if g else b - 1, (g - 1) % NG, UN + u - lag)
                            every = SPARE[l]["every"].get(u)
                            if every == "maxima" and not (last and g == NG - 1):
                                turn_maxima(G + 1, (g + 1) % NG)
                            if every == "contexts" and not (first and g == 0):
                                turn_context(G)
                            if (g, u) in SPARE[l]["next"] and not last:
                                spare(SPARE[l]["next"][g, u], b + 1)
                            if (g, u) in SPARE_LAST[l] and last:
                                spare(SPARE_LAST[l][g, u], b)

                def vexp_needed(b, g, first):
                    return NG if first else NG * b + g + 1

                over_batches(pe, body)
                for u in range(UN - lag, UN):
                    weigh(UN * (NG * B - 1) + u, B - 1, NG - 1, u)
                turn_context(NG * B)

            pe.wait_ge(consts, 10)
            pe.wait_ge(d_w, 16 * LOADS)
            attention_tensor(0)

            def turn_out(b, half):
                pe.wait_ge(ctile_ok, b + 1)
                if not (isinstance(b, int) and b == 0):
                    pe.wait_ge(ctT_ok, b)
                for i in range(KB):
                    last = transpose(m0[:, i * P:(i + 1) * P], xts[0][half][:, i, :], ident[:, :])
                last.then_inc(ct_ps, 1)

            def project(b):
                pe.wait_ge(ctT_ok, b + 1)
                if not (isinstance(b, int) and b == 0):
                    pe.wait_ge(acc0_ok, b)
                mm(banks[6][:, :], wout[:, :], av_s[:, :], start=True, stop=True).then_inc(op_ps, 1)

            def turn_back(b, half):
                pe.wait_ge(acc_ok, E * b + E)
                if not (isinstance(b, int) and b == 0):
                    pe.wait_ge(x1_ok, b)
                for i in range(KB):
                    last = transpose(banks[4][:, i * P:(i + 1) * P], qk_f[:, half, i * P:(i + 1) * P], ident[:, :])
                last.then_inc(yT_ps, 1)

            def out_pair(t, first, last):
                for half in range(2):
                    b = 2 * t + half
                    for e in range(E):
                        if not (first and half == 0 and e < 4):
                            pe.wait_ge(acc_ok, E * b + e - 3)
                        mm(banks[e % 4][:, :], ewT[:, e, :], xnT[:, bass.ds(b * S, S)], start=True, stop=True
                           ).then_inc(ff_ps, 1)
                        if e == 3:
                            if not (first and half == 0):
                                turn_back(b - 1, 1 - half)
                            if not (last and half == 1):
                                turn_out(b + 1, 1 - half)
                    if not (last and half == 1):
                        project(b + 1)

            pe.wait_ge(A[0]["norm_ok"], B * NG)
            pe.wait_ge(ewT_ok, E)
            turn_out(0, 0)
            project(0)
            out_pair(0, True, False)
            with pe.Fori(1, B // 2 - 1) as t:
                out_pair(t, False, False)
            out_pair(B // 2 - 1, False, True)
            turn_back(B - 1, 1)
            attention_tensor(1)

            HALVES = ((0, 0), (0, 1), (1, 0))

            def up(e, n, tb, first):
                for c in range(FC):
                    if not first:
                        pe.wait_ge(hid_ok, FC * (n - 1) + c + 1)
                    for k, (hw, hx) in enumerate(HALVES):
                        last = mm(banks[c][:, :], w_split[:, e % 2, hw, c * P:(c + 1) * P],
                                  xsplit[:, hx, bass.ds(tb * S, S)], start=(k == 0), stop=(k == 2))
                    last.then_inc(up_ps, 1)

            def down(e, n, half):
                pe.wait_ge(h_lo_ok, FC * n + FC)
                pe.wait_ge(add_ok, n + 1)
                for i in range(KB):
                    for c in range(FC):
                        for k, (hh, hw) in enumerate(HALVES):
                            last = mm(banks[4 + half][:, i * P:(i + 1) * P], h_split[half][:, hh, c, i * P:(i + 1) * P],
                                      w_split[:, e % 2, 2 + hw, c * P:(c + 1) * P],
                                      start=(c == 0 and k == 0), stop=(c == FC - 1 and k == 2))
                last.then_inc(dn_ps, 1)

            pe.wait_ge(A[1]["norm_ok"], B * NG)
            pe.wait_ge(x_lo_ok, B)
            pe.wait_ge(w_lo_ok, 2)
            up(0, 0, 0, True)
            for e in range(E + 1):
                with pe.Fori(0, B // 2 - 1) as t:
                    n = B * e + 2 * t
                    up(e, n + 1, 2 * t + 1, False)
                    down(e, n, 0)
                    up(e, n + 2, 2 * t + 2, False)
                    down(e, n + 1, 1)
                n = B * e + B - 2
                up(e, n + 1, B - 1, False)
                down(e, n, 0)
                if e < E:
                    pe.wait_ge(w_lo_ok, 2 * (e + 1) + 2)
                    up(e + 1, n + 2, 0, False)
                down(e, n + 1, 1)

    return nc


_ARGS = {
    "x": "L0_attn_x", "Wqkv": "L0_attn_Wqkv", "bqkv": "L0_attn_bqkv", "Wout": "L0_attn_Wout", "bout": "L0_attn_bout",
    "gate_w": "L0_ffn_gate_w", "gate_b": "L0_ffn_gate_b", "expert_w": "L0_ffn_expert_w", "expert_b": "L0_ffn_expert_b",
    "Wq": "L1_attn_Wq", "bq": "L1_attn_bq", "Wk": "L1_attn_Wk", "bk": "L1_attn_bk", "Wv": "L1_attn_Wv", "bv": "L1_attn_bv",
    "Wg": "L1_attn_Wg", "bg": "L1_attn_bg", "shared_up": "L1_ffn_shared_up", "shared_down": "L1_ffn_shared_down",
    "routed_up": "L1_ffn_routed_up", "routed_down": "L1_ffn_routed_down", "router_w": "L1_ffn_router_w",
}


def kernel(**inputs):
    import concourse.bacc as bacc
    from concourse.bass_utils import run_bass_kernel_spmd

    nc = bacc.Bacc("TRN2", target_bir_lowering=False, num_devices=1)
    arrays, io = {}, {}
    for short, name in _ARGS.items():
        a = np.ascontiguousarray(inputs[name])
        arrays["in_" + short] = a
        io[short] = nc.dram_tensor("in_" + short, a.shape, mybir.dt.from_np(a.dtype), kind="ExternalInput").ap()
    out = nc.dram_tensor("out", (B, S, D), F32, kind="ExternalOutput").ap()
    program(nc, io, out)
    r = run_bass_kernel_spmd(nc, [arrays], core_ids=[0])
    return r.results[0]["out"]
```
